# Optimizing a Trainium2 kernel written in Bass

```python
import numpy as np
import jax
import jax.numpy as jnp

def _softmax(x, axis=-1):
    return jax.nn.softmax(x, axis=axis)

def _gelu(x):
    return jax.nn.gelu(x, approximate=True)

def _silu(x):
    return jax.nn.silu(x)

def _sigmoid(x):
    return jax.nn.sigmoid(x)

def _layernorm(x, axis=-1, eps=1e-05):
    m = jnp.mean(x, axis=axis, keepdims=True)
    v = jnp.var(x, axis=axis, keepdims=True)
    return (x - m) / jnp.sqrt(v + eps)

def _scatter_add(tgt, idx, src, axis=0):
    return tgt.at[idx].add(src)

def _segment_sum(src, seg, n):
    return jax.ops.segment_sum(src, seg, n)
kernel_name = 'mk_dlrm_tower_d1_rec_r8_cf98f0'

def setup_inputs(seed: int=0):
    np.random.seed(seed)
    _w = jnp.asarray

    def _rec_inputs():
        import jax
        import jax.numpy as jnp
        _tk = jax.random.key(seed)
        dense_ctx = jax.random.normal(jax.random.fold_in(_tk, 190), (1024, 16), jnp.float32)
        ids = jnp.stack([jax.random.randint(jax.random.fold_in(_tk, 200 + f), (1024,), 0, v, jnp.int32) for f, v in enumerate([1250, 12500, 1000, 1250, 1000, 1000, 125000, 1000, 1250, 1000, 1000, 1000, 1250, 12500, 1250, 125000, 1250, 12500, 1250, 1250, 125000, 12500, 1000, 125000, 125000, 1000, 1000, 1000, 1000, 1000, 1000, 1250, 1000, 125000, 125000, 12500, 1000, 12500, 1000])], axis=1)
        tbl_0 = 0.05 * jax.random.normal(jax.random.fold_in(_tk, 500 + 0), (1250, 32), jnp.float32)
        tbl_1 = 0.05 * jax.random.normal(jax.random.fold_in(_tk, 500 + 1), (12500, 32), jnp.float32)
        tbl_2 = 0.05 * jax.random.normal(jax.random.fold_in(_tk, 500 + 2), (1000, 32), jnp.float32)
        tbl_3 = 0.05 * jax.random.normal(jax.random.fold_in(_tk, 500 + 3), (1250, 32), jnp.float32)
        tbl_4 = 0.05 * jax.random.normal(jax.random.fold_in(_tk, 500 + 4), (1000, 32), jnp.float32)
        tbl_5 = 0.05 * jax.random.normal(jax.random.fold_in(_tk, 500 + 5), (1000, 32), jnp.float32)
        tbl_6 = 0.05 * jax.random.normal(jax.random.fold_in(_tk, 500 + 6), (125000, 32), jnp.float32)
        tbl_7 = 0.05 * jax.random.normal(jax.random.fold_in(_tk, 500 + 7), (1000, 32), jnp.float32)
        tbl_8 = 0.05 * jax.random.normal(jax.random.fold_in(_tk, 500 + 8), (1250, 32), jnp.float32)
        tbl_9 = 0.05 * jax.random.normal(jax.random.fold_in(_tk, 500 + 9), (1000, 32), jnp.float32)
        tbl_10 = 0.05 * jax.random.normal(jax.random.fold_in(_tk, 500 + 10), (1000, 32), jnp.float32)
        tbl_11 = 0.05 * jax.random.normal(jax.random.fold_in(_tk, 500 + 11), (1000, 32), jnp.float32)
        tbl_12 = 0.05 * jax.random.normal(jax.random.fold_in(_tk, 500 + 12), (1250, 32), jnp.float32)
        tbl_13 = 0.05 * jax.random.normal(jax.random.fold_in(_tk, 500 + 13), (12500, 32), jnp.float32)
        tbl_14 = 0.05 * jax.random.normal(jax.random.fold_in(_tk, 500 + 14), (1250, 32), jnp.float32)
        tbl_15 = 0.05 * jax.random.normal(jax.random.fold_in(_tk, 500 + 15), (125000, 32), jnp.float32)
        tbl_16 = 0.05 * jax.random.normal(jax.random.fold_in(_tk, 500 + 16), (1250, 32), jnp.float32)
        tbl_17 = 0.05 * jax.random.normal(jax.random.fold_in(_tk, 500 + 17), (12500, 32), jnp.float32)
        tbl_18 = 0.05 * jax.random.normal(jax.random.fold_in(_tk, 500 + 18), (1250, 32), jnp.float32)
        tbl_19 = 0.05 * jax.random.normal(jax.random.fold_in(_tk, 500 + 19), (1250, 32), jnp.float32)
        tbl_20 = 0.05 * jax.random.normal(jax.random.fold_in(_tk, 500 + 20), (125000, 32), jnp.float32)
        tbl_21 = 0.05 * jax.random.normal(jax.random.fold_in(_tk, 500 + 21), (12500, 32), jnp.float32)
        tbl_22 = 0.05 * jax.random.normal(jax.random.fold_in(_tk, 500 + 22), (1000, 32), jnp.float32)
        tbl_23 = 0.05 * jax.random.normal(jax.random.fold_in(_tk, 500 + 23), (125000, 32), jnp.float32)
        tbl_24 = 0.05 * jax.random.normal(jax.random.fold_in(_tk, 500 + 24), (125000, 32), jnp.float32)
        tbl_25 = 0.05 * jax.random.normal(jax.random.fold_in(_tk, 500 + 25), (1000, 32), jnp.float32)
        tbl_26 = 0.05 * jax.random.normal(jax.random.fold_in(_tk, 500 + 26), (1000, 32), jnp.float32)
        tbl_27 = 0.05 * jax.random.normal(jax.random.fold_in(_tk, 500 + 27), (1000, 32), jnp.float32)
        tbl_28 = 0.05 * jax.random.normal(jax.random.fold_in(_tk, 500 + 28), (1000, 32), jnp.float32)
        tbl_29 = 0.05 * jax.random.normal(jax.random.fold_in(_tk, 500 + 29), (1000, 32), jnp.float32)
        tbl_30 = 0.05 * jax.random.normal(jax.random.fold_in(_tk, 500 + 30), (1000, 32), jnp.float32)
        tbl_31 = 0.05 * jax.random.normal(jax.random.fold_in(_tk, 500 + 31), (1250, 32), jnp.float32)
        tbl_32 = 0.05 * jax.random.normal(jax.random.fold_in(_tk, 500 + 32), (1000, 32), jnp.float32)
        tbl_33 = 0.05 * jax.random.normal(jax.random.fold_in(_tk, 500 + 33), (125000, 32), jnp.float32)
        tbl_34 = 0.05 * jax.random.normal(jax.random.fold_in(_tk, 500 + 34), (125000, 32), jnp.float32)
        tbl_35 = 0.05 * jax.random.normal(jax.random.fold_in(_tk, 500 + 35), (12500, 32), jnp.float32)
        tbl_36 = 0.05 * jax.random.normal(jax.random.fold_in(_tk, 500 + 36), (1000, 32), jnp.float32)
        tbl_37 = 0.05 * jax.random.normal(jax.random.fold_in(_tk, 500 + 37), (12500, 32), jnp.float32)
        tbl_38 = 0.05 * jax.random.normal(jax.random.fold_in(_tk, 500 + 38), (1000, 32), jnp.float32)
        _rk = jax.random.fold_in(_tk, 7)
        W_top1 = 0.0693375 * jax.random.normal(jax.random.fold_in(_tk, 801), (208, 512), jnp.float32)
        W_top2 = 0.0441942 * jax.random.normal(jax.random.fold_in(_tk, 802), (512, 256), jnp.float32)
        W_top3 = 0.0625 * jax.random.normal(jax.random.fold_in(_tk, 803), (256, 1), jnp.float32)
        b_top1 = jnp.zeros((512,), jnp.float32)
        b_top2 = jnp.zeros((256,), jnp.float32)
        return (dense_ctx, ids, tbl_0, tbl_1, tbl_2, tbl_3, tbl_4, tbl_5, tbl_6, tbl_7, tbl_8, tbl_9, tbl_10, tbl_11, tbl_12, tbl_13, tbl_14, tbl_15, tbl_16, tbl_17, tbl_18, tbl_19, tbl_20, tbl_21, tbl_22, tbl_23, tbl_24, tbl_25, tbl_26, tbl_27, tbl_28, tbl_29, tbl_30, tbl_31, tbl_32, tbl_33, tbl_34, tbl_35, tbl_36, tbl_37, tbl_38, W_top1, b_top1, W_top2, b_top2, W_top3)
    dense_ctx, ids, tbl_0, tbl_1, tbl_2, tbl_3, tbl_4, tbl_5, tbl_6, tbl_7, tbl_8, tbl_9, tbl_10, tbl_11, tbl_12, tbl_13, tbl_14, tbl_15, tbl_16, tbl_17, tbl_18, tbl_19, tbl_20, tbl_21, tbl_22, tbl_23, tbl_24, tbl_25, tbl_26, tbl_27, tbl_28, tbl_29, tbl_30, tbl_31, tbl_32, tbl_33, tbl_34, tbl_35, tbl_36, tbl_37, tbl_38, W_top1, b_top1, W_top2, b_top2, W_top3 = _rec_inputs()

    def _L0_rec_setup():
        import jax, jax.numpy as jnp
        import numpy as np
        LAYER_SIZES = (128, 128)

        def _cin_layer(h0, h, W):
            F0, Fi = (h0.shape[1], h.shape[1])
            K = W.shape[1]
            Wr = W.reshape(F0, Fi, K)
            return jnp.einsum('bid,bjd,ijk->bkd', h0, h, Wr)
        key = jax.random.key(seed)
        k1, k2, k3 = jax.random.split(key, 3)
        B, F0, D = (256, 39, 32)
        F1 = LAYER_SIZES[0] // 2
        x = jax.random.normal(k1, (B, F0, D), dtype=jnp.float32)
        W1 = jax.random.normal(k2, (F0 * F0, LAYER_SIZES[0]), dtype=jnp.float32) * 0.05
        W2 = jax.random.normal(k3, (F0 * F1, LAYER_SIZES[1]), dtype=jnp.float32) * 0.05
        return {'x': x, 'W1': W1, 'W2': W2}
    _L0_rec_all = _L0_rec_setup()
    _L0_rec_in = {k: v for k, v in _L0_rec_all.items() if k in ('W1', 'W2')}
    del _L0_rec_all
    return {'dense_ctx': dense_ctx, 'ids': ids, 'tbl_0': tbl_0, 'tbl_1': tbl_1, 'tbl_2': tbl_2, 'tbl_3': tbl_3, 'tbl_4': tbl_4, 'tbl_5': tbl_5, 'tbl_6': tbl_6, 'tbl_7': tbl_7, 'tbl_8': tbl_8, 'tbl_9': tbl_9, 'tbl_10': tbl_10, 'tbl_11': tbl_11, 'tbl_12': tbl_12, 'tbl_13': tbl_13, 'tbl_14': tbl_14, 'tbl_15': tbl_15, 'tbl_16': tbl_16, 'tbl_17': tbl_17, 'tbl_18': tbl_18, 'tbl_19': tbl_19, 'tbl_20': tbl_20, 'tbl_21': tbl_21, 'tbl_22': tbl_22, 'tbl_23': tbl_23, 'tbl_24': tbl_24, 'tbl_25': tbl_25, 'tbl_26': tbl_26, 'tbl_27': tbl_27, 'tbl_28': tbl_28, 'tbl_29': tbl_29, 'tbl_30': tbl_30, 'tbl_31': tbl_31, 'tbl_32': tbl_32, 'tbl_33': tbl_33, 'tbl_34': tbl_34, 'tbl_35': tbl_35, 'tbl_36': tbl_36, 'tbl_37': tbl_37, 'tbl_38': tbl_38, 'W_top1': W_top1, 'b_top1': b_top1, 'W_top2': W_top2, 'b_top2': b_top2, 'W_top3': W_top3, 'L0_rec_W1': _L0_rec_in['W1'], 'L0_rec_W2': _L0_rec_in['W2']}

def reference(dense_ctx, ids, tbl_0, tbl_1, tbl_2, tbl_3, tbl_4, tbl_5, tbl_6, tbl_7, tbl_8, tbl_9, tbl_10, tbl_11, tbl_12, tbl_13, tbl_14, tbl_15, tbl_16, tbl_17, tbl_18, tbl_19, tbl_20, tbl_21, tbl_22, tbl_23, tbl_24, tbl_25, tbl_26, tbl_27, tbl_28, tbl_29, tbl_30, tbl_31, tbl_32, tbl_33, tbl_34, tbl_35, tbl_36, tbl_37, tbl_38, W_top1, b_top1, W_top2, b_top2, W_top3, L0_rec_W1, L0_rec_W2):
    import jax
    import jax.numpy as jnp

    def _L0_rec_ref(x, W1, W2):
        import jax, jax.numpy as jnp
        import numpy as np
        LAYER_SIZES = (128, 128)

        def _cin_layer(h0, h, W):
            F0, Fi = (h0.shape[1], h.shape[1])
            K = W.shape[1]
            Wr = W.reshape(F0, Fi, K)
            return jnp.einsum('bid,bjd,ijk->bkd', h0, h, Wr)
        conv1 = _cin_layer(x, x, W1)
        half = LAYER_SIZES[0] // 2
        hidden1 = conv1[:, :half, :]
        final1 = conv1[:, half:, :]
        conv2 = _cin_layer(x, hidden1, W2)
        final = jnp.concatenate([final1, conv2], axis=1)
        return jnp.sum(final, axis=2)
    e = jnp.stack([tbl_0[ids[:, 0]], tbl_1[ids[:, 1]], tbl_2[ids[:, 2]], tbl_3[ids[:, 3]], tbl_4[ids[:, 4]], tbl_5[ids[:, 5]], tbl_6[ids[:, 6]], tbl_7[ids[:, 7]], tbl_8[ids[:, 8]], tbl_9[ids[:, 9]], tbl_10[ids[:, 10]], tbl_11[ids[:, 11]], tbl_12[ids[:, 12]], tbl_13[ids[:, 13]], tbl_14[ids[:, 14]], tbl_15[ids[:, 15]], tbl_16[ids[:, 16]], tbl_17[ids[:, 17]], tbl_18[ids[:, 18]], tbl_19[ids[:, 19]], tbl_20[ids[:, 20]], tbl_21[ids[:, 21]], tbl_22[ids[:, 22]], tbl_23[ids[:, 23]], tbl_24[ids[:, 24]], tbl_25[ids[:, 25]], tbl_26[ids[:, 26]], tbl_27[ids[:, 27]], tbl_28[ids[:, 28]], tbl_29[ids[:, 29]], tbl_30[ids[:, 30]], tbl_31[ids[:, 31]], tbl_32[ids[:, 32]], tbl_33[ids[:, 33]], tbl_34[ids[:, 34]], tbl_35[ids[:, 35]], tbl_36[ids[:, 36]], tbl_37[ids[:, 37]], tbl_38[ids[:, 38]]], axis=1)
    z = _L0_rec_ref(e, L0_rec_W1, L0_rec_W2)
    z = z.reshape(z.shape[0], -1)
    h = jnp.concatenate([z, dense_ctx], axis=1)
    h = jnp.maximum(h @ W_top1 + b_top1, 0.0)
    h = jnp.maximum(h @ W_top2 + b_top2, 0.0)
    y = h @ W_top3
    return y

_drawn_inputs = setup_inputs


def setup_inputs(seed=0):
    import zlib

    import numpy as np

    out = dict(_drawn_inputs(seed))
    spreads = {'b_top1': (0.0, 0.1), 'b_top2': (0.0, 0.1)}
    factors = {'tbl_0': 4.842,
     'tbl_1': 4.849,
     'tbl_2': 4.823,
     'tbl_3': 4.798,
     'tbl_4': 5.016,
     'tbl_5': 4.491,
     'tbl_6': 4.757,
     'tbl_7': 4.678,
     'tbl_8': 4.688,
     'tbl_9': 4.972,
     'tbl_10': 5.09,
     'tbl_11': 4.398,
     'tbl_12': 4.803,
     'tbl_13': 4.496,
     'tbl_14': 4.506,
     'tbl_15': 4.779,
     'tbl_16': 4.602,
     'tbl_17': 4.746,
     'tbl_18': 4.927,
     'tbl_19': 5.294,
     'tbl_20': 5.004,
     'tbl_21': 5.139,
     'tbl_22': 5.036,
     'tbl_23': 5.178,
     'tbl_24': 4.857,
     'tbl_25': 4.887,
     'tbl_26': 4.928,
     'tbl_27': 4.653,
     'tbl_28': 4.844,
     'tbl_29': 4.863,
     'tbl_30': 4.388,
     'tbl_31': 4.827,
     'tbl_32': 4.871,
     'tbl_33': 4.546,
     'tbl_34': 4.825,
     'tbl_35': 4.736,
     'tbl_36': 4.842,
     'tbl_37': 4.647,
     'tbl_38': 4.7,
     'L0_rec_W2': 5.439}
    for name, (base, spread) in spreads.items():
        noise = np.random.default_rng([zlib.crc32(name.encode()), seed]).standard_normal(out[name].shape)
        drawn = base * np.exp(spread * noise) if base else spread * noise
        out[name] = jnp.asarray(drawn.astype(out[name].dtype))
    for name, factor in factors.items():
        out[name] = (out[name] * factor).astype(out[name].dtype)
    return out
```

```python
from contextlib import ExitStack

import concourse.bass as bass
import numpy as np
from concourse import mybir

B = 1024
NF = 39
D = 32
K1 = 128
HALF = K1 // 2
K2 = 128
DC = 16
T1, T2 = 512, 256
P = 128

TILES = B // P
PAIRS = 4
GT = 512
GB = GT // D
QUAD = P // D
PARTS = 3
KX = PARTS * NF
HM = (NF + 1) // 2
GI = 2 * HM
GR = HALF + HM * 2
NPROD = 6
NARR = 4
LEFT = 64
CH = 8
CHUNKS = D // CH

ALU = mybir.AluOpType
ACT = mybir.ActivationFunctionType
BF16 = mybir.dt.bfloat16
F32 = mybir.dt.float32
I32 = mybir.dt.int32

ARRAYS_OF = [(0, 1), (0, 2), (1, 2), (0, 3), (1, 3), (2, 3)]
BASE_SETS = [(0, 1, 3, 10), (0, 4, 15, 20), (0, 6, 14, 27)]
LEFT_STEP = 17


def plan_products():
    fields = [[] for _ in range(NARR)]
    for base in BASE_SETS:
        for turn in range(NF):
            for a in range(NARR):
                fields[a].append((base[a] + turn) % NF)
    step = 0
    used = set()
    while len(fields[0]) < P:
        i, j = step, (step + LEFT_STEP) % NF
        if i not in used and j not in used:
            used |= {i, j}
            for a, f in enumerate((i, i, j, j)):
                fields[a].append(f)
        step += 1
    seen, pair = set(), []
    for a, b in ARRAYS_OF:
        rows = []
        for i, j in zip(fields[a], fields[b]):
            key = (min(i, j), max(i, j))
            rows.append(None if key in seen else (i, j))
            seen.add(key)
        pair.append(rows)
    left = [(i, j) for i in range(NF) for j in range(i, NF) if (i, j) not in seen]
    assert len(left) <= LEFT
    return fields, pair, left


def loop_tiles(pair):
    return [t for t in range(NPROD) if any(p and p[0] == p[1] for p in pair[t])]


def constants():
    fields, pair, left = plan_products()
    part = {}
    sel = np.zeros((P, NARR, P), np.float32)
    for a in range(NARR):
        for r, f in enumerate(fields[a]):
            sel[[k * NF + f for k in range(PARTS)], a, r] = 1
    part["sel"] = sel.reshape(P, -1)
    sel_left = np.zeros((P, LEFT), np.float32)
    for r, (i, j) in enumerate(left):
        for k in range(PARTS):
            sel_left[k * NF + i, r] = 1
            sel_left[k * NF + j, r] = 1
    part["sel_left"] = sel_left
    sel_x = np.zeros((P, GI), np.float32)
    for f in range(NF):
        sel_x[[k * NF + f for k in range(PARTS)], (f % 2) * HM + f // 2] = 1
    part["sel_x"] = sel_x
    part["ident"] = np.eye(P, dtype=np.float32)
    part["mask"] = np.repeat((np.arange(P)[:, None] // D == np.arange(QUAD)).astype(np.float32), GI, 1)
    both = np.zeros((2, P, NPROD + 1), np.float32)
    for t in range(NPROD):
        for r, p in enumerate(pair[t]):
            if p:
                both[:, r, t] = (1, 0) if p[0] == p[1] else (1, 1)
    for r, (i, j) in enumerate(left):
        for r2 in (r, r + LEFT):
            both[:, r2, NPROD] = (1, 0) if i == j else (0.5, 0.5)
    part["first"], part["second"] = both
    off = []
    for t in loop_tiles(pair):
        m = np.zeros((P, P), np.float32)
        for r, p in enumerate(pair[t]):
            if p and p[0] == p[1]:
                for e, (i, j) in enumerate(left):
                    if i != j and p[0] in (i, j):
                        m[e, r] = -1
        off.append(m)
    m = np.zeros((P, P), np.float32)
    for r, (s, s2) in enumerate(left):
        if s == s2:
            for e, (i, j) in enumerate(left):
                if i != j and s in (i, j):
                    m[e, [r, r + LEFT]] = -1
    off.append(m)
    part["off"] = np.concatenate(off, 1)
    return part


def columns_of(part):
    at, out = 0, {}
    for name, a in part.items():
        out[name] = (at, at + a.shape[1])
        at += a.shape[1]
    return out, at


class Tile:

    def __init__(self, eng, reg, mul, add, slot, known, first=False, last=False):
        self.eng, self.reg, self.mul, self.add, self.known = eng, reg, mul, add, known
        self.slot, self.first, self.last = slot, first, last

    def linear(self, by, plus):
        if self.reg is None:
            return by * self.add + plus
        key = (by * self.mul, by * self.add + plus)
        if key not in self.known:
            self.known[key] = self.eng.snap(self.reg * key[0] + key[1])
        return self.known[key]

    def pairs(self, q):
        return self.linear(PAIRS, q)

    def starts(self, q, back=1):
        return self.first and q < back

    def tiles(self, n):
        return self.linear(1, n)


def over_tiles(eng, body):
    body(Tile(eng, None, 0, 0, 0, {}, first=True))
    with eng.Fori(0, (TILES - 2) // 2) as it:
        known = {}
        body(Tile(eng, it, 2, 1, 1, known))
        body(Tile(eng, it, 2, 2, 0, known))
    body(Tile(eng, None, 0, TILES - 1, 1, {}, last=True))


def build(nc, ap, out):
    cols, ncols = columns_of(constants())
    loops = loop_tiles(plan_products()[1])
    fixed = loops + [NPROD]

    with ExitStack() as ctx:
        def sb(name, shape, dt=F32):
            return ctx.enter_context(nc.sbuf_tensor(name, shape, dt))

        def bank(name):
            return ctx.enter_context(nc.psum_tensor(name, [P, 512], F32))

        def sem(name):
            return ctx.enter_context(nc.semaphore(name))

        const = sb("const", [P, ncols])
        sel_cols = cols["ident"][1]
        constb = sb("constb", [P, sel_cols], BF16)
        w_first = sb("w_first", [P, NPROD + 1, HALF])
        w_second = sb("w_second", [P, NPROD + 1, HALF])
        w_pair = sb("w_pair", [P, NPROD + 1, HALF])
        w_layer2 = sb("w_layer2", [P, HM, K2])
        w_final1 = sb("w_final1", [P, HM, HALF])
        w_top1_z2 = sb("w_top1_z2", [P, T1])
        w_top1_z1 = sb("w_top1_z1", [HALF + DC, T1])
        w_top2 = sb("w_top2", [P, T1 // P, T2])
        w_top3 = sb("w_top3", [P, T2 // P])
        b_top1 = sb("b_top1", [P, T1 // P])
        b_top2 = sb("b_top2", [P, T2 // P])

        ids = sb("ids", [P, TILES, NF], I32)
        ids_now = sb("ids_now", [P, 2, NF], I32)
        x = sb("x", [P, 2, NF, D])
        x_rest = sb("x_rest", [P, NF, D])
        x_parts = sb("x_parts", [P, D, KX], BF16)
        xt = sb("xt", [KX, 2, P * D], BF16)

        arrays = sb("arrays", [P, 2, NARR, GT])
        prod = sb("prod", [P, 2, 2, NPROD, GT])
        squares = sb("squares", [P, 2, GT])
        hidden_t = sb("hidden_t", [P, GT])
        hx = sb("hx", [P, 2, 2 * QUAD, GR])
        x_apart = sb("x_apart", [P, 2, 2 * QUAD, QUAD * GI])
        m_sum = sb("m_sum", [P, HM, P])
        g_sum = sb("g_sum", [HALF + GI, HM, P])
        z2 = sb("z2", [P, P])
        z1_odd = sb("z1_odd", [HALF, P])
        z1_dense = sb("z1_dense", [HALF + DC, 2, P])
        h1 = sb("h1", [P, T1 // P, P])
        h2 = sb("h2", [P, T2 // P, P])
        y = sb("y", [1, 2, P])

        ring = [bank(f"ring{i}") for i in range(3)]
        acc = [bank("acc_a"), bank("acc_b")]
        misc = bank("misc")
        gram = ctx.enter_context(nc.psum_tensor("gram", [P, 2, 512], F32))

        def cf(name):
            return const[:, cols[name][0]:cols[name][1]]

        def cb(name):
            return constb[0:KX, cols[name][0]:cols[name][1]]

        s_ids = sem("s_ids")
        s_const = sem("s_const")
        s_wpair = sem("s_wpair")
        s_wlayer2 = sem("s_wlayer2")
        s_wtop = sem("s_wtop")
        s_dense = [sem("s_dense0"), sem("s_dense1")]
        gathered = [sem("gathered0"), sem("gathered1")]
        constb_ready = sem("constb_ready")
        zeroed = sem("zeroed")
        w_step = sem("w_step")
        off_done = sem("off_done")
        w_ready = sem("w_ready")
        ids_copied = sem("ids_copied")
        gather_go = sem("gather_go")
        hi_ready = sem("hi_ready")
        x_split = sem("x_split")
        mid_ready = sem("mid_ready")
        lo_ready = sem("lo_ready")
        xtr_done = sem("xtr_done")
        xt_ready = sem("xt_ready")
        z_done = sem("z_done")
        z2_ready = sem("z2_ready")
        z1_ready = sem("z1_ready")
        h1_done = sem("h1_done")
        h1_ready = sem("h1_ready")
        h2_done = sem("h2_done")
        h2_ready = sem("h2_ready")
        y_done = sem("y_done")
        y_ready = sem("y_ready")
        y_out = sem("y_out")
        sel_done = [sem(f"sel_done{j}") for j in range(2 * NARR + 1)]
        array_ready = [sem(f"array_ready{j}") for j in range(2 * NARR)]
        squares_ready = sem("squares_ready")
        prod_ready = [[sem(f"prod_ready{g}{k}") for k in range(NPROD)] for g in range(2)]
        main_done = sem("main_done")
        hidden_ready = [sem("hidden_ready_a"), sem("hidden_ready_b")]
        htt_done = sem("htt_done")
        hx_hidden = sem("hx_hidden")
        xsel_done = sem("xsel_done")
        hx_fields = sem("hx_fields")
        apart_ready = sem("apart_ready")
        gram_done = [sem("gram_done_a"), sem("gram_done_b")]
        m_ready = [sem("m_ready_a"), sem("m_ready_b")]
        g_ready = [sem("g_ready_a"), sem("g_ready_b")]

        block = ctx.enter_context(nc.Block())

        @block.sync
        def _(sp):
            sp.dma_start(ids[:, :, :], ap["ids"].rearrange("(t p) f -> p t f", p=P)).then_inc(s_ids, 16)
            sp.dma_start(const[:, :], ap["const"]).then_inc(s_const, 16)
            sp.dma_start(w_first[:, :, :], ap["w_first"]).then_inc(s_wpair, 16)
            sp.dma_start(w_second[:, :, :], ap["w_second"]).then_inc(s_wpair, 16)
            sp.dma_start(w_layer2[:, :, :], ap["w_layer2"]).then_inc(s_wlayer2, 16)
            sp.dma_start(w_final1[:, :, :], ap["w_final1"]).then_inc(s_wlayer2, 16)
            sp.dma_start(w_top1_z1[0:HALF, :], ap["W_top1"][0:HALF, :]).then_inc(s_wtop, 16)
            sp.dma_start(w_top1_z2[:, :], ap["W_top1"][HALF:HALF + K2, :]).then_inc(s_wtop, 16)
            sp.dma_start(w_top1_z1[HALF:, :], ap["W_top1"][HALF + K2:, :]).then_inc(s_wtop, 16)
            sp.dma_start(w_top2[:, :, :], ap["W_top2"].rearrange("(k p) n -> p k n", p=P)).then_inc(s_wtop, 16)
            sp.dma_start(w_top3[:, :], ap["W_top3"]).then_inc(s_wtop, 16)
            sp.dma_start(b_top1[:, :], ap["b_top1"]).then_inc(s_wtop, 16)
            sp.dma_start(b_top2[:, :], ap["b_top2"]).then_inc(s_wtop, 16)

            def store_y(n):
                sp.wait_ge(y_ready, n.tiles(0))
                slot = 1 - n.slot
                sp.dma_start(out[:, bass.ds(n.linear(P, -P), P)], y[0:1, slot, :]).then_inc(y_out, 16)

            def tile(n):
                if not n.first:
                    store_y(n)
                    sp.wait_ge(y_out, n.linear(16, 0))
                sp.dma_start(z1_dense[HALF:, n.slot, :], ap["dense_t"][:, bass.ds(n.linear(P, 0), P)])\
                  .then_inc(s_dense[n.slot], 16)

            over_tiles(sp, tile)
            store_y(Tile(sp, None, 0, TILES, 0, {}))
            sp.wait_ge(y_out, 16 * TILES)

        @block.gpsimd
        def _(pool):
            pool.wait_ge(s_ids, 16)

            def tile(n):
                if not n.first:
                    pool.wait_ge(x_split, n.tiles(0))
                pool.tensor_copy(ids_now[:, n.slot, :], ids[:, bass.ds(n.tiles(0), 1), :].rearrange("p a f -> p (a f)"))\
                    .then_inc(ids_copied, 1)
                pool.wait_ge(ids_copied, n.tiles(1))
                pool.sem_inc(gather_go, 1)
                for f in range(NF):
                    pool.indirect_dma_start(
                        out=x[:, n.slot, f, :], out_offset=None, in_=ap[f"tbl_{f}"],
                        in_offset=bass.IndirectOffsetOnAxis(ap=ids_now[:, n.slot, f:f + 1], axis=0),
                    ).then_inc(gathered[n.slot], 16)

            over_tiles(pool, tile)

        @block.tensor
        def _(pe):
            def transposes(n, t, c):
                pe.wait_ge(lo_ready, n.tiles(t + 1))
                bf = misc[:, :].bitcast(BF16)
                for i in range(CH):
                    last = nc.tensor.transpose(bf[0:KX, i * P:(i + 1) * P], x_parts[:, c * CH + i, :],
                                               constb[:, cols["ident"][0]:cols["ident"][1]])
                last.then_inc(xtr_done, 1)

            def select(n, q, j):
                slot = (n.slot + q // PAIRS) % 2
                pe.wait_ge(xt_ready, n.pairs(PAIRS * (q // PAIRS) + CHUNKS))
                before = (*array_ready, squares_ready)[j - 3 if j >= 3 else j + 6]
                if j >= 3:
                    pe.wait_ge(before, n.pairs(q + 1))
                elif not n.starts(q):
                    pe.wait_ge(before, n.pairs(q))
                base = (q % PAIRS) * 2 * GT
                if j < 2 * NARR:
                    g, a = divmod(j, NARR)
                    last = nc.tensor.matmul(ring[j % 3][:, :], cb("sel")[:, a * P:(a + 1) * P],
                                            xt[:, slot, base + g * GT:base + (g + 1) * GT], start=True, stop=True)
                else:
                    for g in range(2):
                        last = nc.tensor.matmul(ring[j % 3][g * LEFT:(g + 1) * LEFT, :], cb("sel_left"),
                                                xt[:, slot, base + g * GT:base + (g + 1) * GT], start=True, stop=True)
                last.then_inc(sel_done[j], 1)

            def hidden(n, q, k):
                if k == 0 and not n.starts(q):
                    for g in range(2):
                        pe.wait_ge(hidden_ready[g], n.pairs(q))
                if k == NPROD - 1:
                    pe.wait_ge(squares_ready, n.pairs(q + 1))
                for g in range(2):
                    rows = slice(0, P)
                    if k < NPROD:
                        pe.wait_ge(prod_ready[g][k], n.pairs(q + 1))
                        right = prod[:, q % 2, g, k, :]
                    else:
                        rows = slice(g * LEFT, (g + 1) * LEFT)
                        right = squares[rows, q % 2, :]
                    last = nc.tensor.matmul(acc[g][g * HALF:(g + 1) * HALF, :], w_pair[rows, k, :], right,
                                            start=(k == 0), stop=(k == NPROD))
                if k == NPROD:
                    last.then_inc(main_done, 1)

            def turn_hidden(n, q):
                for g in range(2):
                    pe.wait_ge(hidden_ready[g], n.pairs(q + 1))
                for u in range(QUAD):
                    last = nc.tensor.transpose(misc[:, u * P:(u + 1) * P], hidden_t[:, u * P:(u + 1) * P], cf("ident"))
                last.then_inc(htt_done, 1)

            def turn_fields(n, q):
                for u in range(2 * QUAD):
                    at = q * 2 * GT + (u % 2) * GT + (u // 2) * P
                    last = nc.tensor.matmul(misc[:, u * GI:(u + 1) * GI], xt[:, n.slot, at:at + P], cb("sel_x"),
                                            start=True, stop=True)
                last.then_inc(xsel_done, 1)

            def gram_sums(n, q, g):
                pe.wait_ge(hx_hidden, n.pairs(q + 1))
                pe.wait_ge(hx_fields, n.pairs(q + 1))
                pe.wait_ge(apart_ready, n.pairs(q + 1))
                if g == 1 or not n.starts(q):
                    pe.wait_ge(m_ready[1 - g], n.pairs(q + g))
                    pe.wait_ge(g_ready[1 - g], n.pairs(q + g))
                for u in range(QUAD):
                    last = nc.tensor.matmul(gram[0:GR, u // 2, (u % 2) * QUAD * GI:(u % 2 + 1) * QUAD * GI],
                                            hx[:, q % 2, 2 * u + g, :], x_apart[:, q % 2, 2 * u + g, :],
                                            start=True, stop=True)
                last.then_inc(gram_done[g], 1)

            def layer2(n):
                pe.wait_ge(m_ready[1], n.pairs(0))
                pe.wait_ge(g_ready[1], n.pairs(0))
                for m in range(HM):
                    nc.tensor.matmul(misc[:, 0:P], w_layer2[:, m, :], m_sum[:, m, :],
                                     start=(m == 0), stop=(m == HM - 1))
                for m in range(HM):
                    c = m % 2
                    last = nc.tensor.matmul(misc[c * HALF:(c + 1) * HALF, P:2 * P], w_final1[0:HALF + GI, m, :],
                                            g_sum[:, m, :], start=(m < 2), stop=(m >= HM - 2))
                last.then_inc(z_done, 1)

            def tower1(n):
                slot = 1 - n.slot
                pe.wait_ge(z2_ready, n.tiles(0))
                pe.wait_ge(z1_ready, n.tiles(0))
                pe.wait_ge(s_dense[slot], dense_loads(n))
                for c in range(T1 // P):
                    nc.tensor.matmul(misc[:, c * P:(c + 1) * P], w_top1_z2[:, c * P:(c + 1) * P], z2[:, :],
                                     start=True, stop=False)
                    last = nc.tensor.matmul(misc[:, c * P:(c + 1) * P], w_top1_z1[:, c * P:(c + 1) * P],
                                            z1_dense[:, slot, :], start=False, stop=True)
                last.then_inc(h1_done, 1)

            def tower2(n):
                pe.wait_ge(h1_ready, n.tiles(0))
                for c in range(T2 // P):
                    for k in range(T1 // P):
                        last = nc.tensor.matmul(misc[:, c * P:(c + 1) * P], w_top2[:, k, c * P:(c + 1) * P], h1[:, k, :],
                                                start=(k == 0), stop=(k == T1 // P - 1))
                last.then_inc(h2_done, 1)

            def tower3(n):
                pe.wait_ge(h2_ready, n.tiles(0))
                for k in range(T2 // P):
                    last = nc.tensor.matmul(misc[0:1, 0:P], w_top3[:, k:k + 1], h2[:, k, :],
                                            start=(k == 0), stop=(k == T2 // P - 1))
                last.then_inc(y_done, 1)

            def dense_loads(n):
                if n.reg is None:
                    return 16 * ((n.add - 1) // 2 + 1)
                return n.eng.snap(n.reg * 16 + 16 * ((n.add - 1) // 2 + 1))

            pe.wait_ge(w_step, 1)
            for c in range(len(fixed)):
                last = nc.tensor.matmul(misc[:, c * HALF:(c + 1) * HALF],
                                        cf("off")[0:LEFT, c * P:(c + 1) * P], w_pair[0:LEFT, NPROD, :],
                                        start=True, stop=True)
            last.then_inc(off_done, 1)
            pe.wait_ge(constb_ready, 1)
            first = Tile(pe, None, 0, 0, 0, {}, first=True)
            for c in range(CHUNKS):
                if c == 0:
                    pe.wait_ge(w_ready, 1)
                else:
                    pe.wait_ge(xt_ready, c)
                transposes(first, 0, c)
            for j in range(2 * NARR + 1):
                select(first, 0, j)
            pe.wait_ge(s_wlayer2, 32)
            pe.wait_ge(s_wtop, 7 * 16)

            def tail_gram(n, q, g):
                if not (n.first and q == 0):
                    gram_sums(n, q - 1, g)

            def pair(n, q):
                more = not (n.last and q == PAIRS - 1)
                late = n.first and q == PAIRS - 1
                turn = n.first and q == 3 or not n.first and not n.last and q == 2
                tower = not n.first and q == 1

                def ahead(*js):
                    if more and not late:
                        for j in js:
                            select(n, q + 1, j)

                ahead(0, 1, 2)
                hidden(n, q, 0)
                ahead(3, 4)
                if not (n.first and q == 0):
                    if q == 2 and not n.first:
                        pe.wait_ge(y_ready, n.tiles(0))
                    elif q == 3 and not n.first and not n.last:
                        pe.wait_ge(xt_ready, n.pairs(2 * PAIRS))
                    else:
                        pe.wait_ge(hx_fields, n.pairs(q))
                    turn_hidden(n, q - 1)
                hidden(n, q, 1)
                if tower:
                    pe.wait_ge(hx_hidden, n.pairs(q))
                    layer2(n)
                if turn:
                    pe.wait_ge(hx_hidden, n.pairs(q))
                    transposes(n, 1, 0)
                ahead(5)
                hidden(n, q, 2)
                tail_gram(n, q, 0)
                ahead(6)
                if tower:
                    pe.wait_ge(z2_ready, n.tiles(0))
                    pe.wait_ge(z1_ready, n.tiles(0))
                elif turn:
                    pe.wait_ge(xt_ready, n.pairs(CHUNKS + 1))
                elif n.first and q == 0:
                    pe.wait_ge(xt_ready, CHUNKS)
                else:
                    pe.wait_ge(hx_hidden, n.pairs(q))
                turn_fields(n, q)
                hidden(n, q, 3)
                ahead(7, 8)
                if tower:
                    pe.wait_ge(hx_fields, n.pairs(q + 1))
                    tower1(n)
                if turn:
                    pe.wait_ge(hx_fields, n.pairs(q + 1))
                    transposes(n, 1, 1)
                tail_gram(n, q, 1)
                hidden(n, q, 4)
                if tower:
                    tower2(n)
                if turn:
                    pe.wait_ge(xt_ready, n.pairs(CHUNKS + 2))
                    transposes(n, 1, 2)
                hidden(n, q, 5)
                if tower:
                    tower3(n)
                if turn:
                    pe.wait_ge(xt_ready, n.pairs(CHUNKS + 3))
                    transposes(n, 1, 3)
                hidden(n, q, 6)
                if late:
                    for j in range(2 * NARR + 1):
                        select(n, q + 1, j)

            def tile(n):
                for q in range(PAIRS):
                    pair(n, q)

            over_tiles(pe, tile)
            end = Tile(pe, None, 0, TILES, 0, {})
            pe.wait_ge(hx_fields, end.pairs(0))
            turn_hidden(end, -1)
            gram_sums(end, -1, 0)
            gram_sums(end, -1, 1)
            layer2(end)
            tower1(end)
            tower2(end)
            tower3(end)

        @block.scalar
        def _(act):
            copy = ACT.Copy
            act.wait_ge(s_const, 16)
            nc.scalar.activation(constb[:, :], const[:, 0:sel_cols], copy).then_inc(constb_ready, 1)

            def parts_of(slot, k):
                return x_parts[:, :, k * NF:(k + 1) * NF].rearrange("p d f -> p f d")

            def split_hi(n, t):
                slot = (n.slot + t) % 2
                act.wait_ge(gathered[slot], gather_count(n, t))
                if not n.starts(t):
                    act.wait_ge(xtr_done, n.pairs(PAIRS * t))
                nc.scalar.activation(parts_of(slot, 0), x[:, slot, :, :], copy).then_inc(hi_ready, 1)

            def gather_count(n, t):
                if n.reg is None:
                    return 16 * NF * ((n.add + t) // 2 + 1)
                return n.eng.snap(n.reg * (16 * NF) + 16 * NF * ((n.add + t) // 2 + 1))

            def split_mid(n, t):
                act.wait_ge(x_split, n.tiles(t + 2))
                nc.scalar.activation(parts_of(0, 1), x_rest[:, :, :], copy).then_inc(mid_ready, 1)

            def keep_transposes(n, t, c):
                slot = (n.slot + t) % 2
                act.wait_ge(xtr_done, n.pairs(PAIRS * t + c + 1))
                bf = misc[:, :].bitcast(BF16)[0:KX, :].rearrange("p (d b) -> p b d", d=CH)
                to = xt[:, slot, :].rearrange("p (b d) -> p b d", d=D)[:, :, c * CH:(c + 1) * CH]
                nc.scalar.activation(to, bf, copy).then_inc(xt_ready, 1)

            def keep_array(n, q, j):
                act.wait_ge(sel_done[j], n.pairs(q + 1))
                if j < 2 * NARR:
                    g, a = divmod(j, NARR)
                    if not n.starts(q):
                        act.wait_ge(prod_ready[g][NPROD - 1], n.pairs(q))
                    nc.scalar.activation(arrays[:, g, a, :], ring[j % 3][:, :], copy).then_inc(array_ready[j], 1)
                else:
                    if not n.starts(q, back=2):
                        act.wait_ge(main_done, n.pairs(q - 1))
                    nc.scalar.activation(squares[:, q % 2, :], ring[j % 3][:, :], ACT.Square)\
                        .then_inc(squares_ready, 1)

            def keep_hidden(n, q):
                act.wait_ge(main_done, n.pairs(q + 1))
                for g in range(2):
                    rows = slice(g * HALF, (g + 1) * HALF)
                    nc.scalar.activation(hidden_t[rows, :], acc[g][rows, :], copy).then_inc(hidden_ready[g], 1)

            def keep_turned_hidden(n, q):
                act.wait_ge(htt_done, n.pairs(q + 1))
                nc.scalar.activation(hx[:, q % 2, :, 0:HALF], misc[:, :].rearrange("p (u j) -> p u j", j=HALF), copy)\
                    .then_inc(hx_hidden, 1)

            def keep_fields(n, q):
                act.wait_ge(xsel_done, n.pairs(q + 1))
                nc.scalar.activation(hx[:, q % 2, :, HALF:GR],
                                     misc[:, 0:2 * QUAD * GI].rearrange("p (u i) -> p u i", i=GI), copy)\
                    .then_inc(hx_fields, 1)

            def keep_m(n, q, g):
                act.wait_ge(gram_done[g], n.pairs(q + 1))
                for par in range(2):
                    for h in range(2):
                        src = gram[0:HALF, h, 0:2 * QUAD * GI].rearrange("p (b i) -> p b i", i=GI)
                        at = (q % PAIRS) * 2 * GB + g * GB + h * 2 * QUAD
                        last = nc.scalar.activation(
                            m_sum[par * HALF:(par + 1) * HALF, :, at:at + 2 * QUAD].rearrange("p m b -> p b m"),
                            src[:, :, par * HM:(par + 1) * HM], copy)
                last.then_inc(m_ready[g], 1)

            def keep_z(n):
                act.wait_ge(z_done, n.tiles(0))
                nc.scalar.activation(z1_odd[:, :], misc[HALF:P, P:2 * P], copy)
                nc.scalar.activation(z2[:, :], misc[:, 0:P], copy).then_inc(z2_ready, 1)

            def relu1(n):
                act.wait_ge(h1_done, n.tiles(0))
                for c in range(T1 // P):
                    last = nc.scalar.activation(h1[:, c, :], misc[:, c * P:(c + 1) * P], ACT.Relu,
                                                bias=b_top1[:, c:c + 1])
                last.then_inc(h1_ready, 1)

            def relu2(n):
                act.wait_ge(h2_done, n.tiles(0))
                for c in range(T2 // P):
                    last = nc.scalar.activation(h2[:, c, :], misc[:, c * P:(c + 1) * P], ACT.Relu,
                                                bias=b_top2[:, c:c + 1])
                last.then_inc(h2_ready, 1)

            def keep_y(n):
                act.wait_ge(y_done, n.tiles(0))
                nc.scalar.activation(y[0:1, 1 - n.slot, :], misc[0:1, 0:P], copy).then_inc(y_ready, 1)

            first = Tile(act, None, 0, 0, 0, {}, first=True)
            split_hi(first, 0)
            split_mid(first, 0)
            for c in range(CHUNKS):
                keep_transposes(first, 0, c)
            for j in range(2 * NARR + 1):
                keep_array(first, 0, j)
            act.wait_ge(s_wtop, 7 * 16)

            def pair(n, q):
                more = not (n.last and q == PAIRS - 1)
                late = n.first and q == PAIRS - 1
                turn = n.first and q == 3 or not n.first and not n.last and q == 2
                tower = not n.first and q == 1
                start = n.first and q == 2 or not n.first and not n.last and q == 1
                behind = not (n.first and q == 0)

                def ahead(*js):
                    if more and not late:
                        for j in js:
                            keep_array(n, q + 1, j)

                if behind:
                    keep_hidden(n, q - 1)
                if turn:
                    split_mid(n, 1)
                if start and not n.first:
                    split_hi(n, 1)
                ahead(0, 1, 2, 3, 4)
                if behind:
                    keep_turned_hidden(n, q - 1)
                if tower:
                    keep_z(n)
                if turn:
                    keep_transposes(n, 1, 0)
                ahead(5)
                if behind:
                    keep_m(n, q - 1, 0)
                ahead(6)
                keep_fields(n, q)
                ahead(7, 8)
                if tower:
                    relu1(n)
                if turn:
                    keep_transposes(n, 1, 1)
                if behind:
                    keep_m(n, q - 1, 1)
                if tower:
                    relu2(n)
                if turn:
                    keep_transposes(n, 1, 2)
                if tower:
                    keep_y(n)
                if turn:
                    keep_transposes(n, 1, 3)
                if start and n.first:
                    split_hi(n, 1)
                if late:
                    for j in range(2 * NARR + 1):
                        keep_array(n, q + 1, j)

            def tile(n):
                for q in range(PAIRS):
                    pair(n, q)

            over_tiles(act, tile)
            end = Tile(act, None, 0, TILES, 0, {})
            keep_hidden(end, -1)
            keep_turned_hidden(end, -1)
            keep_m(end, -1, 0)
            keep_m(end, -1, 1)
            keep_z(end)
            relu1(end)
            relu2(end)
            keep_y(end)

        @block.vector
        def _(dve):
            nc.vector.memset(g_sum[:, :, :], 0.0).then_inc(zeroed, 1)
            nc.vector.memset(y[:, :, :], 0.0).then_inc(x_split, 1)
            dve.wait_ge(s_const, 16)
            dve.wait_ge(s_wpair, 32)
            steps = 0
            for k in range(NPROD, -1, -1):
                nc.vector.tensor_scalar(w_second[:, k, :], w_second[:, k, :], cf("second")[:, k:k + 1], None, ALU.mult)\
                  .then_inc(zeroed, 1)
                steps += 1
                dve.wait_ge(zeroed, steps + 1)
                nc.vector.scalar_tensor_tensor(out=w_pair[:, k, :], in0=w_first[:, k, :], scalar=cf("first")[:, k:k + 1],
                                               in1=w_second[:, k, :], op0=ALU.mult, op1=ALU.add).then_inc(w_step, 1)
            dve.wait_ge(off_done, 1)
            dve.wait_ge(w_step, NPROD + 1)
            for c, k in enumerate(fixed):
                last = nc.vector.tensor_tensor(w_pair[:, k, :], w_pair[:, k, :], misc[:, c * HALF:(c + 1) * HALF], ALU.add)
            last.then_inc(w_ready, 1)

            def parts_of(k):
                return x_parts[:, :, k * NF:(k + 1) * NF].rearrange("p d f -> p f d")

            def split_rest(n, t):
                slot = (n.slot + t) % 2
                dve.wait_ge(hi_ready, n.tiles(t + 1))
                nc.vector.tensor_tensor(x_rest[:, :, :], x[:, slot, :, :], parts_of(0), ALU.subtract)\
                  .then_inc(x_split, 1)

            def split_lo(n, t):
                dve.wait_ge(mid_ready, n.tiles(t + 1))
                nc.vector.tensor_tensor(parts_of(2), x_rest[:, :, :], parts_of(1), ALU.subtract).then_inc(lo_ready, 1)

            def multiply(n, q, g, *ks):
                for k in ks:
                    a, b = ARRAYS_OF[k]
                    dve.wait_ge(array_ready[g * NARR + a], n.pairs(q + 1))
                    dve.wait_ge(array_ready[g * NARR + b], n.pairs(q + 1))
                    if not n.starts(q, back=2):
                        dve.wait_ge(main_done, n.pairs(q - 1))
                    nc.vector.tensor_tensor(prod[:, q % 2, g, k, :], arrays[:, g, a, :], arrays[:, g, b, :], ALU.mult)\
                      .then_inc(prod_ready[g][k], 1)

            def set_apart(n, q):
                dve.wait_ge(hx_fields, n.pairs(q + 1))
                src = hx[:, q % 2, :, HALF:GR]
                mask = cf("mask").rearrange("p (b i) -> p b i", i=GI)
                for b in range(QUAD):
                    last = nc.vector.tensor_tensor(
                        x_apart[:, q % 2, :, b * GI:(b + 1) * GI], src,
                        mask[:, b:b + 1, :].to_broadcast([P, 2 * QUAD, GI]), ALU.mult)
                last.then_inc(apart_ready, 1)

            def keep_g(n, q, g):
                dve.wait_ge(gram_done[g], n.pairs(q + 1))
                for par in range(2):
                    for h in range(2):
                        src = gram[HALF:GR, h, 0:2 * QUAD * GI].rearrange("p (b i) -> p b i", i=GI)
                        at = (q % PAIRS) * 2 * GB + g * GB + h * 2 * QUAD
                        last = nc.vector.tensor_copy(
                            g_sum[par * HALF:par * HALF + GI, :, at:at + 2 * QUAD].rearrange("p m b -> p b m"),
                            src[:, :, par * HM:(par + 1) * HM])
                last.then_inc(g_ready[g], 1)

            def add_z1(n):
                dve.wait_ge(z2_ready, n.tiles(0))
                nc.vector.tensor_tensor(z1_dense[0:HALF, 1 - n.slot, :], misc[0:HALF, P:2 * P], z1_odd[:, :], ALU.add)\
                  .then_inc(z1_ready, 1)

            first = Tile(dve, None, 0, 0, 0, {}, first=True)
            split_rest(first, 0)
            split_lo(first, 0)
            for g in range(2):
                multiply(first, 0, g, *range(NPROD))

            def pair(n, q):
                more = not (n.last and q == PAIRS - 1)
                late = n.first and q == PAIRS - 1
                turn = n.first and q == 3 or not n.first and not n.last and q == 2
                tower = not n.first and q == 1
                start = n.first and q == 2 or not n.first and not n.last and q == 1
                behind = not (n.first and q == 0)

                def ahead(g, *ks):
                    if more and not late:
                        multiply(n, q + 1, g, *ks)

                if turn:
                    split_lo(n, 1)
                ahead(0, 0, 1, 2)
                if start and not n.first:
                    split_rest(n, 1)
                ahead(0, 3, 4, 5)
                if tower:
                    add_z1(n)
                if behind:
                    keep_g(n, q - 1, 0)
                ahead(1, 0, 1, 2)
                set_apart(n, q)
                ahead(1, 3, 4, 5)
                if behind:
                    keep_g(n, q - 1, 1)
                if start and n.first:
                    split_rest(n, 1)
                if late:
                    for g in range(2):
                        multiply(n, q + 1, g, *range(NPROD))

            def tile(n):
                for q in range(PAIRS):
                    pair(n, q)

            over_tiles(dve, tile)
            end = Tile(dve, None, 0, TILES, 0, {})
            keep_g(end, -1, 0)
            keep_g(end, -1, 1)
            add_z1(end)


def kernel(**inputs):
    import concourse.bacc as bacc
    from concourse.bass_utils import run_bass_kernel_spmd

    def rows(a):
        return np.asarray(a)

    _, pair, left = plan_products()
    w1 = rows(inputs["L0_rec_W1"]).reshape(NF, NF, K1)
    w_first = np.zeros((P, NPROD + 1, HALF), np.float32)
    w_second = np.zeros((P, NPROD + 1, HALF), np.float32)
    placed = [(t, r, p) for t in range(NPROD) for r, p in enumerate(pair[t]) if p]
    placed += [(NPROD, r + c, p) for r, p in enumerate(left) for c in (0, LEFT)]
    for t, r, (i, j) in placed:
        w_first[r, t] = w1[i, j, :HALF]
        w_second[r, t] = w1[j, i, :HALF]
    w2 = rows(inputs["L0_rec_W2"]).reshape(NF, HALF, K2)
    w_layer2 = np.zeros((P, HM, K2), np.float32)
    w_final1 = np.zeros((P, HM, HALF), np.float32)
    for i in range(NF):
        par, m = i % 2, i // 2
        w_layer2[par * HALF:(par + 1) * HALF, m] = w2[i]
        for par2 in range(2):
            of = w1[i, par2::2, HALF:]
            at = par * HALF + par2 * HM
            w_final1[at:at + of.shape[0], m] = of
    arrays = {
        "ids": rows(inputs["ids"]),
        "const": np.concatenate(list(constants().values()), 1),
        "w_first": w_first, "w_second": w_second, "w_layer2": w_layer2, "w_final1": w_final1,
        "W_top1": rows(inputs["W_top1"]), "W_top2": rows(inputs["W_top2"]),
        "W_top3": np.ascontiguousarray(rows(inputs["W_top3"]).reshape(T2 // P, P).T),
        "b_top1": np.ascontiguousarray(rows(inputs["b_top1"]).reshape(T1 // P, P).T),
        "b_top2": np.ascontiguousarray(rows(inputs["b_top2"]).reshape(T2 // P, P).T),
        "dense_t": np.ascontiguousarray(rows(inputs["dense_ctx"]).T),
    }
    for f in range(NF):
        arrays[f"tbl_{f}"] = rows(inputs[f"tbl_{f}"])

    nc = bacc.Bacc("TRN2", target_bir_lowering=False, num_devices=1)
    ap = {k: nc.dram_tensor(f"in_{k}", a.shape, mybir.dt.from_np(a.dtype), kind="ExternalInput").ap()
          for k, a in arrays.items()}
    out = nc.dram_tensor("out", (1, B), F32, kind="ExternalOutput").ap()
    build(nc, ap, out)
    r = run_bass_kernel_spmd(nc, [{f"in_{k}": a for k, a in arrays.items()}], core_ids=[0])
    return r.results[0]["out"].reshape(B, 1)
```

```python
from contextlib import ExitStack

import concourse.bass as bass
import numpy as np
from concourse import mybir

B = 1024
NF = 39
D = 32
K1 = 128
HALF = K1 // 2
K2 = 128
DC = 16
T1, T2 = 512, 256
P = 128

TILES = B // P
PAIRS = 4
GT = 512
GB = GT // D
QUAD = P // D
PARTS = 3
KX = PARTS * NF
HM = (NF + 1) // 2
GI = 2 * HM
GR = HALF + HM * 2
NPROD = 6
NARR = 4
LEFT = 64
CH = 8
CHUNKS = D // CH
HEAD_FIELDS = [(0, 17), (17, 32), (32, NF)]

ALU = mybir.AluOpType
ACT = mybir.ActivationFunctionType
BF16 = mybir.dt.bfloat16
F32 = mybir.dt.float32
I32 = mybir.dt.int32

ARRAYS_OF = [(0, 1), (0, 2), (1, 2), (0, 3), (1, 3), (2, 3)]
BASE_SETS = [(0, 1, 3, 10), (0, 4, 15, 20), (0, 6, 14, 27)]
LEFT_STEP = 17


def plan_products():
    fields = [[] for _ in range(NARR)]
    for base in BASE_SETS:
        for turn in range(NF):
            for a in range(NARR):
                fields[a].append((base[a] + turn) % NF)
    step = 0
    used = set()
    while len(fields[0]) < P:
        i, j = step, (step + LEFT_STEP) % NF
        if i not in used and j not in used:
            used |= {i, j}
            for a, f in enumerate((i, i, j, j)):
                fields[a].append(f)
        step += 1
    seen, pair = set(), []
    for a, b in ARRAYS_OF:
        rows = []
        for i, j in zip(fields[a], fields[b]):
            key = (min(i, j), max(i, j))
            rows.append(None if key in seen else (i, j))
            seen.add(key)
        pair.append(rows)
    left = [(i, j) for i in range(NF) for j in range(i, NF) if (i, j) not in seen]
    assert len(left) <= LEFT
    return fields, pair, left


def loop_tiles(pair):
    return [t for t in range(NPROD) if any(p and p[0] == p[1] for p in pair[t])]


def constants():
    fields, pair, left = plan_products()
    part = {}
    sel = np.zeros((P, NARR, P), np.float32)
    for a in range(NARR):
        for r, f in enumerate(fields[a]):
            sel[[k * NF + f for k in range(PARTS)], a, r] = 1
    part["sel"] = sel.reshape(P, -1)
    sel_left = np.zeros((P, LEFT), np.float32)
    for r, (i, j) in enumerate(left):
        for k in range(PARTS):
            sel_left[k * NF + i, r] = 1
            sel_left[k * NF + j, r] = 1
    part["sel_left"] = sel_left
    sel_x = np.zeros((P, GI), np.float32)
    for f in range(NF):
        sel_x[[k * NF + f for k in range(PARTS)], (f % 2) * HM + f // 2] = 1
    part["sel_x"] = sel_x
    part["ident"] = np.eye(P, dtype=np.float32)
    part["mask"] = np.repeat((np.arange(P)[:, None] // D == np.arange(QUAD)).astype(np.float32), GI, 1)
    both = np.zeros((2, P, NPROD + 1), np.float32)
    for t in range(NPROD):
        for r, p in enumerate(pair[t]):
            if p:
                both[:, r, t] = (1, 0) if p[0] == p[1] else (1, 1)
    for r, (i, j) in enumerate(left):
        for r2 in (r, r + LEFT):
            both[:, r2, NPROD] = (1, 0) if i == j else (0.5, 0.5)
    part["first"], part["second"] = both
    off = []
    for t in loop_tiles(pair):
        m = np.zeros((P, P), np.float32)
        for r, p in enumerate(pair[t]):
            if p and p[0] == p[1]:
                for e, (i, j) in enumerate(left):
                    if i != j and p[0] in (i, j):
                        m[e, r] = -1
        off.append(m)
    m = np.zeros((P, P), np.float32)
    for r, (s, s2) in enumerate(left):
        if s == s2:
            for e, (i, j) in enumerate(left):
                if i != j and s in (i, j):
                    m[e, [r, r + LEFT]] = -1
    off.append(m)
    part["off"] = np.concatenate(off, 1)
    return part


def columns_of(part):
    at, out = 0, {}
    for name, a in part.items():
        out[name] = (at, at + a.shape[1])
        at += a.shape[1]
    return out, at


class Tile:

    def __init__(self, eng, reg, mul, add, slot, known, first=False, last=False):
        self.eng, self.reg, self.mul, self.add, self.known = eng, reg, mul, add, known
        self.slot, self.first, self.last = slot, first, last
        self.turn = None if last else PAIRS - 1 if first else PAIRS - 2

    def linear(self, by, plus):
        if self.reg is None:
            return by * self.add + plus
        key = (by * self.mul, by * self.add + plus)
        if key not in self.known:
            self.known[key] = self.eng.snap(self.reg * key[0] + key[1])
        return self.known[key]

    def pairs(self, q):
        return self.linear(PAIRS, q)

    def starts(self, q, back=1):
        return self.first and q < back

    def tiles(self, n):
        return self.linear(1, n)


def over_tiles(eng, body):
    body(Tile(eng, None, 0, 0, 0, {}, first=True))
    with eng.Fori(0, (TILES - 2) // 2) as it:
        known = {}
        body(Tile(eng, it, 2, 1, 1, known))
        body(Tile(eng, it, 2, 2, 0, known))
    body(Tile(eng, None, 0, TILES - 1, 1, {}, last=True))


def build(nc, ap, out):
    cols, ncols = columns_of(constants())
    loops = loop_tiles(plan_products()[1])
    fixed = loops + [NPROD]

    with ExitStack() as ctx:
        def sb(name, shape, dt=F32):
            return ctx.enter_context(nc.sbuf_tensor(name, shape, dt))

        def bank(name):
            return ctx.enter_context(nc.psum_tensor(name, [P, 512], F32))

        def sem(name):
            return ctx.enter_context(nc.semaphore(name))

        const = sb("const", [P, ncols])
        sel_cols = cols["ident"][1]
        constb = sb("constb", [P, sel_cols], BF16)
        w_first = sb("w_first", [P, NPROD + 1, HALF])
        w_second = sb("w_second", [P, NPROD + 1, HALF])
        w_pair = sb("w_pair", [P, NPROD + 1, HALF])
        w_layer2 = sb("w_layer2", [P, HM, K2])
        w_final1 = sb("w_final1", [P, HM, HALF])
        w_top1_z2 = sb("w_top1_z2", [P, T1])
        w_top1_z1 = sb("w_top1_z1", [HALF + DC, T1])
        w_top2 = sb("w_top2", [P, T1 // P, T2])
        w_top3 = sb("w_top3", [P, T2 // P])
        b_top1 = sb("b_top1", [P, T1 // P])
        b_top2 = sb("b_top2", [P, T2 // P])

        ids = sb("ids", [P, TILES, NF], I32)
        ids_now = sb("ids_now", [P, 2, NF], I32)
        x = sb("x", [P, 2, NF, D])
        x_rest = sb("x_rest", [P, NF, D])
        x_parts = sb("x_parts", [P, D, KX], BF16)
        xt = sb("xt", [KX, 2, P * D], BF16)

        arrays = sb("arrays", [P, 2, NARR, GT])
        prod = sb("prod", [P, 2, 2, NPROD, GT])
        squares = sb("squares", [P, 2, GT])
        hidden_t = sb("hidden_t", [P, GT])
        hx = sb("hx", [P, 2, 2 * QUAD, GR])
        x_apart = sb("x_apart", [P, 2, 2 * QUAD, QUAD * GI])
        m_sum = sb("m_sum", [P, HM, P])
        g_sum = sb("g_sum", [HALF + GI, HM, P])
        z2 = sb("z2", [P, P])
        z1_odd = sb("z1_odd", [HALF, P])
        z1_dense = sb("z1_dense", [HALF + DC, 2, P])
        h1 = sb("h1", [P, T1 // P, P])
        h2 = sb("h2", [P, T2 // P, P])
        y = sb("y", [1, 2, P])

        ring = [bank(f"ring{i}") for i in range(3)]
        acc = [bank("acc_a"), bank("acc_b")]
        misc = bank("misc")
        gram = ctx.enter_context(nc.psum_tensor("gram", [P, 2, 512], F32))

        def cf(name):
            return const[:, cols[name][0]:cols[name][1]]

        def cb(name):
            return constb[0:KX, cols[name][0]:cols[name][1]]

        s_ids = sem("s_ids")
        s_const = sem("s_const")
        s_wpair = sem("s_wpair")
        s_wlayer2 = sem("s_wlayer2")
        s_wtop = sem("s_wtop")
        s_dense = [sem("s_dense0"), sem("s_dense1")]
        gathered = [sem("gathered0"), sem("gathered1")]
        head_gathered = [sem(f"head_gathered{k}") for k in range(len(HEAD_FIELDS))]
        constb_ready = sem("constb_ready")
        zeroed = sem("zeroed")
        w_step = sem("w_step")
        off_done = sem("off_done")
        w_ready = sem("w_ready")
        ids_copied = sem("ids_copied")
        gather_go = sem("gather_go")
        head_hi = sem("head_hi")
        head_rest = sem("head_rest")
        head_mid = sem("head_mid")
        head_lo = sem("head_lo")
        hi_ready = sem("hi_ready")
        x_split = sem("x_split")
        mid_ready = sem("mid_ready")
        lo_ready = sem("lo_ready")
        xtr_done = sem("xtr_done")
        xt_ready = sem("xt_ready")
        z_done = sem("z_done")
        z2_ready = sem("z2_ready")
        z1_ready = sem("z1_ready")
        h1_done = sem("h1_done")
        h1_ready = sem("h1_ready")
        h2_done = sem("h2_done")
        h2_ready = sem("h2_ready")
        y_done = sem("y_done")
        y_ready = sem("y_ready")
        y_out = sem("y_out")
        sel_done = [sem(f"sel_done{j}") for j in range(2 * NARR + 1)]
        array_ready = [sem(f"array_ready{j}") for j in range(2 * NARR)]
        squares_ready = sem("squares_ready")
        prod_ready = [[sem(f"prod_ready{g}{k}") for k in range(NPROD)] for g in range(2)]
        main_done = sem("main_done")
        hidden_ready = [sem("hidden_ready_a"), sem("hidden_ready_b")]
        htt_done = sem("htt_done")
        hx_hidden = sem("hx_hidden")
        xsel_done = sem("xsel_done")
        hx_fields = sem("hx_fields")
        apart_ready = sem("apart_ready")
        gram_done = [sem("gram_done_a"), sem("gram_done_b")]
        m_ready = [sem("m_ready_a"), sem("m_ready_b")]
        g_ready = [sem("g_ready_a"), sem("g_ready_b")]

        def chunk_bank(n, c):
            return (ring[c] if n.first and c < 3 else misc)[:, :].bitcast(BF16)

        block = ctx.enter_context(nc.Block())

        @block.sync
        def _(sp):
            sp.dma_start(ids[:, :, :], ap["ids"].rearrange("(t p) f -> p t f", p=P)).then_inc(s_ids, 16)
            sp.dma_start(const[:, :], ap["const"]).then_inc(s_const, 16)
            sp.dma_start(w_first[:, :, :], ap["w_first"]).then_inc(s_wpair, 16)
            sp.dma_start(w_second[:, :, :], ap["w_second"]).then_inc(s_wpair, 16)
            sp.dma_start(w_layer2[:, :, :], ap["w_layer2"]).then_inc(s_wlayer2, 16)
            sp.dma_start(w_final1[:, :, :], ap["w_final1"]).then_inc(s_wlayer2, 16)
            sp.dma_start(w_top1_z1[0:HALF, :], ap["W_top1"][0:HALF, :]).then_inc(s_wtop, 16)
            sp.dma_start(w_top1_z2[:, :], ap["W_top1"][HALF:HALF + K2, :]).then_inc(s_wtop, 16)
            sp.dma_start(w_top1_z1[HALF:, :], ap["W_top1"][HALF + K2:, :]).then_inc(s_wtop, 16)
            sp.dma_start(w_top2[:, :, :], ap["W_top2"].rearrange("(k p) n -> p k n", p=P)).then_inc(s_wtop, 16)
            sp.dma_start(w_top3[:, :], ap["W_top3"]).then_inc(s_wtop, 16)
            sp.dma_start(b_top1[:, :], ap["b_top1"]).then_inc(s_wtop, 16)
            sp.dma_start(b_top2[:, :], ap["b_top2"]).then_inc(s_wtop, 16)

            def store_y(n):
                sp.wait_ge(y_ready, n.tiles(0))
                slot = 1 - n.slot
                sp.dma_start(out[:, bass.ds(n.linear(P, -P), P)], y[0:1, slot, :]).then_inc(y_out, 16)

            def tile(n):
                if not n.first:
                    store_y(n)
                    sp.wait_ge(y_out, n.linear(16, 0))
                sp.dma_start(z1_dense[HALF:, n.slot, :], ap["dense_t"][:, bass.ds(n.linear(P, 0), P)])\
                  .then_inc(s_dense[n.slot], 16)

            over_tiles(sp, tile)
            store_y(Tile(sp, None, 0, TILES, 0, {}))
            sp.wait_ge(y_out, 16 * TILES)

        @block.gpsimd
        def _(pool):
            pool.wait_ge(s_ids, 16)

            def tile(n):
                if not n.first:
                    pool.wait_ge(x_split, n.tiles(0))
                pool.tensor_copy(ids_now[:, n.slot, :], ids[:, bass.ds(n.tiles(0), 1), :].rearrange("p a f -> p (a f)"))\
                    .then_inc(ids_copied, 1)
                pool.wait_ge(ids_copied, n.tiles(1))
                pool.sem_inc(gather_go, 1)
                for f in range(NF):
                    done = gathered[n.slot]
                    if n.first:
                        done = head_gathered[[f < hi for lo, hi in HEAD_FIELDS].index(True)]
                    pool.indirect_dma_start(
                        out=x[:, n.slot, f, :], out_offset=None, in_=ap[f"tbl_{f}"],
                        in_offset=bass.IndirectOffsetOnAxis(ap=ids_now[:, n.slot, f:f + 1], axis=0),
                    ).then_inc(done, 16)

            over_tiles(pool, tile)

        @block.tensor
        def _(pe):
            def transposes(n, t, c):
                pe.wait_ge(lo_ready, n.tiles(t + 1))
                bf = chunk_bank(n, c)
                for i in range(CH):
                    last = nc.tensor.transpose(bf[0:KX, i * P:(i + 1) * P], x_parts[:, c * CH + i, :],
                                               constb[:, cols["ident"][0]:cols["ident"][1]])
                last.then_inc(xtr_done, 1)

            def select(n, q, j):
                slot = (n.slot + q // PAIRS) % 2
                pe.wait_ge(xt_ready, n.pairs(PAIRS * (q // PAIRS) + CHUNKS))
                before = (*array_ready, squares_ready)[j - 3 if j >= 3 else j + 6]
                if j >= 3:
                    pe.wait_ge(before, n.pairs(q + 1))
                elif not n.starts(q):
                    pe.wait_ge(before, n.pairs(q))
                base = (q % PAIRS) * 2 * GT
                if j < 2 * NARR:
                    g, a = divmod(j, NARR)
                    last = nc.tensor.matmul(ring[j % 3][:, :], cb("sel")[:, a * P:(a + 1) * P],
                                            xt[:, slot, base + g * GT:base + (g + 1) * GT], start=True, stop=True)
                else:
                    for g in range(2):
                        last = nc.tensor.matmul(ring[j % 3][g * LEFT:(g + 1) * LEFT, :], cb("sel_left"),
                                                xt[:, slot, base + g * GT:base + (g + 1) * GT], start=True, stop=True)
                last.then_inc(sel_done[j], 1)

            def hidden(n, q, k):
                if k == 0 and not n.starts(q):
                    for g in range(2):
                        pe.wait_ge(hidden_ready[g], n.pairs(q))
                if k == NPROD - 1:
                    pe.wait_ge(squares_ready, n.pairs(q + 1))
                for g in range(2):
                    rows = slice(0, P)
                    if k < NPROD:
                        pe.wait_ge(prod_ready[g][k], n.pairs(q + 1))
                        right = prod[:, q % 2, g, k, :]
                    else:
                        rows = slice(g * LEFT, (g + 1) * LEFT)
                        right = squares[rows, q % 2, :]
                    last = nc.tensor.matmul(acc[g][g * HALF:(g + 1) * HALF, :], w_pair[rows, k, :], right,
                                            start=(k == 0), stop=(k == NPROD))
                if k == NPROD:
                    last.then_inc(main_done, 1)

            def turn_hidden(n, q):
                for g in range(2):
                    pe.wait_ge(hidden_ready[g], n.pairs(q + 1))
                for u in range(QUAD):
                    last = nc.tensor.transpose(misc[:, u * P:(u + 1) * P], hidden_t[:, u * P:(u + 1) * P], cf("ident"))
                last.then_inc(htt_done, 1)

            def turn_fields(n, q):
                for u in range(2 * QUAD):
                    at = q * 2 * GT + (u % 2) * GT + (u // 2) * P
                    last = nc.tensor.matmul(misc[:, u * GI:(u + 1) * GI], xt[:, n.slot, at:at + P], cb("sel_x"),
                                            start=True, stop=True)
                last.then_inc(xsel_done, 1)

            def gram_sums(n, q, g):
                pe.wait_ge(hx_hidden, n.pairs(q + 1))
                pe.wait_ge(hx_fields, n.pairs(q + 1))
                pe.wait_ge(apart_ready, n.pairs(q + 1))
                if g == 1 or not n.starts(q):
                    pe.wait_ge(m_ready[1 - g], n.pairs(q + g))
                    pe.wait_ge(g_ready[1 - g], n.pairs(q + g))
                for u in range(QUAD):
                    last = nc.tensor.matmul(gram[0:GR, u // 2, (u % 2) * QUAD * GI:(u % 2 + 1) * QUAD * GI],
                                            hx[:, q % 2, 2 * u + g, :], x_apart[:, q % 2, 2 * u + g, :],
                                            start=True, stop=True)
                last.then_inc(gram_done[g], 1)

            def layer2(n):
                pe.wait_ge(m_ready[1], n.pairs(0))
                pe.wait_ge(g_ready[1], n.pairs(0))
                for m in range(HM):
                    nc.tensor.matmul(misc[:, 0:P], w_layer2[:, m, :], m_sum[:, m, :],
                                     start=(m == 0), stop=(m == HM - 1))
                for m in range(HM):
                    c = m % 2
                    last = nc.tensor.matmul(misc[c * HALF:(c + 1) * HALF, P:2 * P], w_final1[0:HALF + GI, m, :],
                                            g_sum[:, m, :], start=(m < 2), stop=(m >= HM - 2))
                last.then_inc(z_done, 1)

            def tower1(n):
                slot = 1 - n.slot
                pe.wait_ge(z1_ready, n.tiles(0))
                pe.wait_ge(s_dense[slot], dense_loads(n))
                for c in range(T1 // P):
                    nc.tensor.matmul(misc[:, c * P:(c + 1) * P], w_top1_z2[:, c * P:(c + 1) * P], z2[:, :],
                                     start=True, stop=False)
                    last = nc.tensor.matmul(misc[:, c * P:(c + 1) * P], w_top1_z1[:, c * P:(c + 1) * P],
                                            z1_dense[:, slot, :], start=False, stop=True)
                last.then_inc(h1_done, 1)

            def tower2(n):
                pe.wait_ge(h1_ready, n.tiles(0))
                for c in range(T2 // P):
                    for k in range(T1 // P):
                        last = nc.tensor.matmul(misc[:, c * P:(c + 1) * P], w_top2[:, k, c * P:(c + 1) * P], h1[:, k, :],
                                                start=(k == 0), stop=(k == T1 // P - 1))
                last.then_inc(h2_done, 1)

            def tower3(n):
                pe.wait_ge(h2_ready, n.tiles(0))
                for k in range(T2 // P):
                    last = nc.tensor.matmul(misc[0:1, 0:P], w_top3[:, k:k + 1], h2[:, k, :],
                                            start=(k == 0), stop=(k == T2 // P - 1))
                last.then_inc(y_done, 1)

            def dense_loads(n):
                if n.reg is None:
                    return 16 * ((n.add - 1) // 2 + 1)
                return n.eng.snap(n.reg * 16 + 16 * ((n.add - 1) // 2 + 1))

            pe.wait_ge(w_step, 1)
            for c in range(len(fixed)):
                last = nc.tensor.matmul(misc[:, c * HALF:(c + 1) * HALF],
                                        cf("off")[0:LEFT, c * P:(c + 1) * P], w_pair[0:LEFT, NPROD, :],
                                        start=True, stop=True)
            last.then_inc(off_done, 1)
            pe.wait_ge(constb_ready, 1)
            first = Tile(pe, None, 0, 0, 0, {}, first=True)
            pe.wait_ge(w_ready, 1)
            for c in range(CHUNKS):
                transposes(first, 0, c)
            for j in range(2 * NARR + 1):
                select(first, 0, j)
            pe.wait_ge(s_wlayer2, 32)
            pe.wait_ge(s_wtop, 7 * 16)

            def pair(n, q):
                more = not (n.last and q == PAIRS - 1)
                late = n.first and q == PAIRS - 1
                turn = q == n.turn
                tower = not n.first

                def ahead(*js):
                    if more and not late:
                        for j in js:
                            select(n, q + 1, j)

                def behind(*js):
                    if late:
                        for j in js:
                            select(n, q + 1, j)

                if not n.starts(q, back=2):
                    gram_sums(n, q - 2, 1)
                ahead(0, 1, 2)
                if not n.starts(q):
                    turn_hidden(n, q - 1)
                hidden(n, q, 0)
                if late:
                    pe.wait_ge(array_ready[6], n.pairs(q + 1))
                    transposes(n, 1, 0)
                    pe.wait_ge(array_ready[7], n.pairs(q + 1))
                    transposes(n, 1, 1)
                ahead(3, 4)
                hidden(n, q, 1)
                if late:
                    pe.wait_ge(squares_ready, n.pairs(q + 1))
                    transposes(n, 1, 2)
                    pe.wait_ge(hx_hidden, n.pairs(q))
                    transposes(n, 1, 3)
                elif turn:
                    pe.wait_ge(hx_hidden, n.pairs(q))
                    transposes(n, 1, 0)
                elif tower and q == 3:
                    pe.wait_ge(hx_hidden, n.pairs(q))
                    tower2(n)
                hidden(n, q, 2)
                ahead(5, 6, 7)
                if tower and q == 1:
                    pe.wait_ge(hx_hidden, n.pairs(q))
                    layer2(n)
                elif turn and not late:
                    pe.wait_ge(xt_ready, n.pairs(CHUNKS + 1))
                    transposes(n, 1, 1)
                hidden(n, q, 3)
                if not n.starts(q):
                    gram_sums(n, q - 1, 0)
                if tower and q == 1:
                    pe.wait_ge(z2_ready, n.tiles(0))
                elif late:
                    pe.wait_ge(xt_ready, n.pairs(CHUNKS + 4))
                elif turn:
                    pe.wait_ge(xt_ready, n.pairs(CHUNKS + 2))
                elif tower and q == 3:
                    pe.wait_ge(h2_ready, n.tiles(0))
                elif n.starts(q):
                    pe.wait_ge(xt_ready, CHUNKS)
                else:
                    pe.wait_ge(hx_hidden, n.pairs(q))
                turn_fields(n, q)
                behind(0, 1, 2)
                hidden(n, q, 4)
                if tower and q == 1:
                    pe.wait_ge(hx_fields, n.pairs(q + 1))
                    tower1(n)
                elif turn and not late:
                    pe.wait_ge(hx_fields, n.pairs(q + 1))
                    transposes(n, 1, 2)
                elif tower and q == 3:
                    pe.wait_ge(hx_fields, n.pairs(q + 1))
                    tower3(n)
                ahead(8)
                behind(3, 4)
                hidden(n, q, 5)
                if turn and not late:
                    pe.wait_ge(xt_ready, n.pairs(CHUNKS + 3))
                    transposes(n, 1, 3)
                behind(5, 6)
                hidden(n, q, 6)
                behind(7, 8)

            def tile(n):
                for q in range(PAIRS):
                    pair(n, q)

            over_tiles(pe, tile)
            end = Tile(pe, None, 0, TILES, 0, {})
            gram_sums(end, -2, 1)
            turn_hidden(end, -1)
            gram_sums(end, -1, 0)
            gram_sums(end, -1, 1)
            layer2(end)
            pe.wait_ge(z2_ready, end.tiles(0))
            tower1(end)
            tower2(end)
            tower3(end)

        @block.scalar
        def _(act):
            copy = ACT.Copy
            act.wait_ge(s_const, 16)
            nc.scalar.activation(constb[:, :], const[:, 0:sel_cols], copy).then_inc(constb_ready, 1)

            def parts_of(slot, k):
                return x_parts[:, :, k * NF:(k + 1) * NF].rearrange("p d f -> p f d")

            def split_head(k):
                a, b = HEAD_FIELDS[k]
                act.wait_ge(head_gathered[k], 16 * (b - a))
                nc.scalar.activation(parts_of(0, 0)[:, a:b, :], x[:, 0, a:b, :], copy).then_inc(head_hi, 1)
                if k == len(HEAD_FIELDS) - 1:
                    act.wait_ge(x_split, 2)
                else:
                    act.wait_ge(head_rest, k + 1)
                nc.scalar.activation(parts_of(0, 1)[:, a:b, :], x_rest[:, a:b, :], copy).then_inc(head_mid, 1)

            def split_hi(n, t):
                slot = (n.slot + t) % 2
                act.wait_ge(gathered[slot], gather_count(n, t))
                act.wait_ge(xtr_done, n.pairs(PAIRS * t))
                nc.scalar.activation(parts_of(slot, 0), x[:, slot, :, :], copy).then_inc(hi_ready, 1)

            def gather_count(n, t):
                if n.reg is None:
                    return 16 * NF * ((n.add + t + 1) // 2)
                return n.eng.snap(n.reg * (16 * NF) + 16 * NF * ((n.add + t + 1) // 2))

            def split_mid(n, t):
                act.wait_ge(x_split, n.tiles(t + 2))
                nc.scalar.activation(parts_of(0, 1), x_rest[:, :, :], copy).then_inc(mid_ready, 1)

            def keep_transposes(n, t, c):
                slot = (n.slot + t) % 2
                act.wait_ge(xtr_done, n.pairs(PAIRS * t + c + 1))
                bf = chunk_bank(n, c)[0:KX, :].rearrange("p (d b) -> p b d", d=CH)
                to = xt[:, slot, :].rearrange("p (b d) -> p b d", d=D)[:, :, c * CH:(c + 1) * CH]
                nc.scalar.activation(to, bf, copy).then_inc(xt_ready, 1)

            def keep_array(n, q, j):
                act.wait_ge(sel_done[j], n.pairs(q + 1))
                if j < 2 * NARR:
                    g, a = divmod(j, NARR)
                    if not n.starts(q):
                        act.wait_ge(prod_ready[g][NPROD - 1], n.pairs(q))
                    nc.scalar.activation(arrays[:, g, a, :], ring[j % 3][:, :], copy).then_inc(array_ready[j], 1)
                else:
                    if not n.starts(q, back=2):
                        act.wait_ge(main_done, n.pairs(q - 1))
                    nc.scalar.activation(squares[:, q % 2, :], ring[j % 3][:, :], ACT.Square)\
                        .then_inc(squares_ready, 1)

            def keep_hidden(n, q):
                act.wait_ge(main_done, n.pairs(q + 1))
                for g in range(2):
                    rows = slice(g * HALF, (g + 1) * HALF)
                    nc.scalar.activation(hidden_t[rows, :], acc[g][rows, :], copy).then_inc(hidden_ready[g], 1)

            def keep_turned_hidden(n, q):
                act.wait_ge(htt_done, n.pairs(q + 1))
                nc.scalar.activation(hx[:, q % 2, :, 0:HALF], misc[:, :].rearrange("p (u j) -> p u j", j=HALF), copy)\
                    .then_inc(hx_hidden, 1)

            def keep_fields(n, q):
                act.wait_ge(xsel_done, n.pairs(q + 1))
                nc.scalar.activation(hx[:, q % 2, :, HALF:GR],
                                     misc[:, 0:2 * QUAD * GI].rearrange("p (u i) -> p u i", i=GI), copy)\
                    .then_inc(hx_fields, 1)

            def keep_m(n, q, g):
                act.wait_ge(gram_done[g], n.pairs(q + 1))
                src = gram[0:HALF, :, 0:2 * QUAD * GI].rearrange("p h (b i) -> p h b i", i=GI)
                at = (q % PAIRS) * 2 * GB + g * GB
                for par in range(2):
                    to = m_sum[par * HALF:(par + 1) * HALF, :, at:at + GB].rearrange("p m (h b) -> p h b m", h=2)
                    last = nc.scalar.activation(to, src[:, :, :, par * HM:(par + 1) * HM], copy)
                last.then_inc(m_ready[g], 1)

            def keep_z(n):
                act.wait_ge(z_done, n.tiles(0))
                nc.scalar.activation(z1_odd[:, :], misc[HALF:P, P:2 * P], copy)
                nc.scalar.activation(z1_dense[0:HALF, 1 - n.slot, :], misc[0:HALF, P:2 * P], copy)
                nc.scalar.activation(z2[:, :], misc[:, 0:P], copy).then_inc(z2_ready, 1)

            def relu1(n):
                act.wait_ge(h1_done, n.tiles(0))
                for c in range(T1 // P):
                    last = nc.scalar.activation(h1[:, c, :], misc[:, c * P:(c + 1) * P], ACT.Relu,
                                                bias=b_top1[:, c:c + 1])
                last.then_inc(h1_ready, 1)

            def relu2(n):
                act.wait_ge(h2_done, n.tiles(0))
                for c in range(T2 // P):
                    last = nc.scalar.activation(h2[:, c, :], misc[:, c * P:(c + 1) * P], ACT.Relu,
                                                bias=b_top2[:, c:c + 1])
                last.then_inc(h2_ready, 1)

            def keep_y(n):
                act.wait_ge(y_done, n.tiles(0))
                nc.scalar.activation(y[0:1, 1 - n.slot, :], misc[0:1, 0:P], copy).then_inc(y_ready, 1)

            first = Tile(act, None, 0, 0, 0, {}, first=True)
            for k in range(len(HEAD_FIELDS)):
                split_head(k)
            keep_transposes(first, 0, 0)
            keep_transposes(first, 0, 2)
            for j in range(2 * NARR + 1):
                keep_array(first, 0, j)
            act.wait_ge(s_wtop, 7 * 16)

            def pair(n, q):
                more = not (n.last and q == PAIRS - 1)
                late = n.first and q == PAIRS - 1
                turn = q == n.turn
                tower = not n.first
                start = n.turn is not None and q == n.turn - 1

                def ahead(*js):
                    if more and not late:
                        for j in js:
                            keep_array(n, q + 1, j)

                def behind(*js):
                    if late:
                        for j in js:
                            keep_array(n, q + 1, j)

                if not n.starts(q):
                    keep_hidden(n, q - 1)
                ahead(0, 1, 2)
                if not n.starts(q):
                    keep_turned_hidden(n, q - 1)
                ahead(3, 4)
                if not n.starts(q, back=2):
                    keep_m(n, q - 2, 1)
                if turn:
                    keep_transposes(n, 1, 0)
                elif tower and q == 3:
                    relu2(n)
                if late:
                    keep_transposes(n, 1, 2)
                ahead(5)
                if start and not n.first:
                    split_hi(n, 1)
                if turn and not late:
                    keep_transposes(n, 1, 1)
                ahead(6, 7)
                if start and not n.first:
                    split_mid(n, 1)
                if tower and q == 1:
                    keep_z(n)
                keep_fields(n, q)
                behind(0, 1)
                if not n.starts(q):
                    keep_m(n, q - 1, 0)
                if tower and q == 1:
                    relu1(n)
                if turn and not late:
                    keep_transposes(n, 1, 2)
                if tower and q == 3:
                    keep_y(n)
                ahead(8)
                if turn and not late:
                    keep_transposes(n, 1, 3)
                if start and n.first:
                    split_hi(n, 1)
                    split_mid(n, 1)
                behind(2, 3, 4, 5, 6, 7, 8)

            def tile(n):
                for q in range(PAIRS):
                    pair(n, q)

            over_tiles(act, tile)
            end = Tile(act, None, 0, TILES, 0, {})
            keep_hidden(end, -1)
            keep_turned_hidden(end, -1)
            keep_m(end, -2, 1)
            keep_m(end, -1, 0)
            keep_m(end, -1, 1)
            keep_z(end)
            relu1(end)
            relu2(end)
            keep_y(end)

        @block.vector
        def _(dve):
            nc.vector.memset(g_sum[:, :, :], 0.0).then_inc(zeroed, 1)
            nc.vector.memset(y[:, :, :], 0.0).then_inc(x_split, 1)
            dve.wait_ge(s_const, 16)
            dve.wait_ge(s_wpair, 32)
            steps = 0
            for k in range(NPROD, -1, -1):
                nc.vector.tensor_scalar(w_second[:, k, :], w_second[:, k, :], cf("second")[:, k:k + 1], None, ALU.mult)\
                  .then_inc(zeroed, 1)
                steps += 1
                dve.wait_ge(zeroed, steps + 1)
                nc.vector.scalar_tensor_tensor(out=w_pair[:, k, :], in0=w_first[:, k, :], scalar=cf("first")[:, k:k + 1],
                                               in1=w_second[:, k, :], op0=ALU.mult, op1=ALU.add).then_inc(w_step, 1)
            dve.wait_ge(off_done, 1)
            dve.wait_ge(w_step, NPROD + 1)
            for c, k in enumerate(fixed):
                last = nc.vector.tensor_tensor(w_pair[:, k, :], w_pair[:, k, :], misc[:, c * HALF:(c + 1) * HALF], ALU.add)
            last.then_inc(w_ready, 1)

            def parts_of(k):
                return x_parts[:, :, k * NF:(k + 1) * NF].rearrange("p d f -> p f d")

            def split_head(k):
                a, b = HEAD_FIELDS[k]
                last = k == len(HEAD_FIELDS) - 1
                dve.wait_ge(head_hi, k + 1)
                nc.vector.tensor_tensor(x_rest[:, a:b, :], x[:, 0, a:b, :], parts_of(0)[:, a:b, :], ALU.subtract)\
                  .then_inc(x_split if last else head_rest, 1)
                dve.wait_ge(head_mid, k + 1)
                nc.vector.tensor_tensor(parts_of(2)[:, a:b, :], x_rest[:, a:b, :], parts_of(1)[:, a:b, :], ALU.subtract)\
                  .then_inc(lo_ready if last else head_lo, 1)

            def keep_transposes(n, t, c):
                dve.wait_ge(xtr_done, n.pairs(PAIRS * t + c + 1))
                bf = chunk_bank(n, c)[0:KX, :].rearrange("p (d b) -> p b d", d=CH)
                to = xt[:, (n.slot + t) % 2, :].rearrange("p (b d) -> p b d", d=D)[:, :, c * CH:(c + 1) * CH]
                nc.vector.tensor_copy(to, bf).then_inc(xt_ready, 1)

            def split_rest(n, t):
                slot = (n.slot + t) % 2
                dve.wait_ge(hi_ready, n.tiles(t))
                nc.vector.tensor_tensor(x_rest[:, :, :], x[:, slot, :, :], parts_of(0), ALU.subtract)\
                  .then_inc(x_split, 1)

            def split_lo(n, t):
                dve.wait_ge(mid_ready, n.tiles(t))
                nc.vector.tensor_tensor(parts_of(2), x_rest[:, :, :], parts_of(1), ALU.subtract).then_inc(lo_ready, 1)

            def multiply(n, q, g, *ks):
                for k in ks:
                    a, b = ARRAYS_OF[k]
                    dve.wait_ge(array_ready[g * NARR + a], n.pairs(q + 1))
                    dve.wait_ge(array_ready[g * NARR + b], n.pairs(q + 1))
                    if not n.starts(q, back=2):
                        dve.wait_ge(main_done, n.pairs(q - 1))
                    nc.vector.tensor_tensor(prod[:, q % 2, g, k, :], arrays[:, g, a, :], arrays[:, g, b, :], ALU.mult)\
                      .then_inc(prod_ready[g][k], 1)

            def set_apart(n, q):
                dve.wait_ge(hx_fields, n.pairs(q + 1))
                src = hx[:, q % 2, :, HALF:GR]
                mask = cf("mask").rearrange("p (b i) -> p b i", i=GI)
                for b in range(QUAD):
                    last = nc.vector.tensor_tensor(
                        x_apart[:, q % 2, :, b * GI:(b + 1) * GI], src,
                        mask[:, b:b + 1, :].to_broadcast([P, 2 * QUAD, GI]), ALU.mult)
                last.then_inc(apart_ready, 1)

            def keep_g(n, q, g):
                dve.wait_ge(gram_done[g], n.pairs(q + 1))
                src = gram[HALF:GR, :, 0:2 * QUAD * GI].rearrange("p h (b i) -> p h b i", i=GI)
                at = (q % PAIRS) * 2 * GB + g * GB
                for par in range(2):
                    to = g_sum[par * HALF:par * HALF + GI, :, at:at + GB].rearrange("p m (h b) -> p h b m", h=2)
                    last = nc.vector.tensor_copy(to, src[:, :, :, par * HM:(par + 1) * HM])
                last.then_inc(g_ready[g], 1)

            def add_z1(n):
                dve.wait_ge(z2_ready, n.tiles(0))
                z1 = z1_dense[0:HALF, 1 - n.slot, :]
                nc.vector.tensor_tensor(z1, z1, z1_odd[:, :], ALU.add)\
                  .then_inc(z1_ready, 1)

            first = Tile(dve, None, 0, 0, 0, {}, first=True)
            for k in range(len(HEAD_FIELDS)):
                split_head(k)
            keep_transposes(first, 0, 1)
            keep_transposes(first, 0, 3)
            for g in range(2):
                multiply(first, 0, g, *range(NPROD))

            def pair(n, q):
                more = not (n.last and q == PAIRS - 1)
                late = n.first and q == PAIRS - 1
                turn = q == n.turn
                tower = not n.first
                start = n.turn is not None and q == n.turn - 1

                def ahead(g, *ks):
                    if more and not late:
                        multiply(n, q + 1, g, *ks)

                ahead(0, 0)
                if not n.starts(q, back=2):
                    keep_g(n, q - 2, 1)
                ahead(0, 1, 2)
                if start and not n.first:
                    split_rest(n, 1)
                ahead(0, 3, 4, 5)
                if late:
                    keep_transposes(n, 1, 1)
                    keep_transposes(n, 1, 3)
                ahead(1, 0, 1, 2, 3)
                if tower and q == 1:
                    ahead(1, 4, 5)
                    add_z1(n)
                if not n.starts(q):
                    keep_g(n, q - 1, 0)
                if not (tower and q == 1):
                    ahead(1, 4, 5)
                set_apart(n, q)
                if start and n.first:
                    split_rest(n, 1)
                if start:
                    split_lo(n, 1)
                if late:
                    for g in range(2):
                        multiply(n, q + 1, g, *range(NPROD))

            def tile(n):
                for q in range(PAIRS):
                    pair(n, q)

            over_tiles(dve, tile)
            end = Tile(dve, None, 0, TILES, 0, {})
            keep_g(end, -2, 1)
            keep_g(end, -1, 0)
            keep_g(end, -1, 1)
            add_z1(end)


def kernel(**inputs):
    import concourse.bacc as bacc
    from concourse.bass_utils import run_bass_kernel_spmd

    def rows(a):
        return np.asarray(a)

    _, pair, left = plan_products()
    w1 = rows(inputs["L0_rec_W1"]).reshape(NF, NF, K1)
    w_first = np.zeros((P, NPROD + 1, HALF), np.float32)
    w_second = np.zeros((P, NPROD + 1, HALF), np.float32)
    placed = [(t, r, p) for t in range(NPROD) for r, p in enumerate(pair[t]) if p]
    placed += [(NPROD, r + c, p) for r, p in enumerate(left) for c in (0, LEFT)]
    for t, r, (i, j) in placed:
        w_first[r, t] = w1[i, j, :HALF]
        w_second[r, t] = w1[j, i, :HALF]
    w2 = rows(inputs["L0_rec_W2"]).reshape(NF, HALF, K2)
    w_layer2 = np.zeros((P, HM, K2), np.float32)
    w_final1 = np.zeros((P, HM, HALF), np.float32)
    for i in range(NF):
        par, m = i % 2, i // 2
        w_layer2[par * HALF:(par + 1) * HALF, m] = w2[i]
        for par2 in range(2):
            of = w1[i, par2::2, HALF:]
            at = par * HALF + par2 * HM
            w_final1[at:at + of.shape[0], m] = of
    arrays = {
        "ids": rows(inputs["ids"]),
        "const": np.concatenate(list(constants().values()), 1),
        "w_first": w_first, "w_second": w_second, "w_layer2": w_layer2, "w_final1": w_final1,
        "W_top1": rows(inputs["W_top1"]), "W_top2": rows(inputs["W_top2"]),
        "W_top3": np.ascontiguousarray(rows(inputs["W_top3"]).reshape(T2 // P, P).T),
        "b_top1": np.ascontiguousarray(rows(inputs["b_top1"]).reshape(T1 // P, P).T),
        "b_top2": np.ascontiguousarray(rows(inputs["b_top2"]).reshape(T2 // P, P).T),
        "dense_t": np.ascontiguousarray(rows(inputs["dense_ctx"]).T),
    }
    for f in range(NF):
        arrays[f"tbl_{f}"] = rows(inputs[f"tbl_{f}"])

    nc = bacc.Bacc("TRN2", target_bir_lowering=False, num_devices=1)
    ap = {k: nc.dram_tensor(f"in_{k}", a.shape, mybir.dt.from_np(a.dtype), kind="ExternalInput").ap()
          for k, a in arrays.items()}
    out = nc.dram_tensor("out", (1, B), F32, kind="ExternalOutput").ap()
    build(nc, ap, out)
    r = run_bass_kernel_spmd(nc, [{f"in_{k}": a for k, a in arrays.items()}], core_ids=[0])
    return r.results[0]["out"].reshape(B, 1)
```

```python
from contextlib import ExitStack

import concourse.bass as bass
import numpy as np
from concourse import mybir

B = 1024
NF = 39
D = 32
K1 = 128
HALF = K1 // 2
K2 = 128
DC = 16
T1, T2 = 512, 256
P = 128

TILES = B // P
PAIRS = 4
GT = 512
GB = GT // D
QUAD = P // D
PARTS = 3
COPIES = P // NF
KX = COPIES * NF
HM = (NF + 1) // 2
IN_HALF = (HM, NF - HM)
GI = NF
GR = HALF + GI
GQ = 32
BLOCKS = [(0, 12, 0, 0, 0), (12, 24, 0, GQ, 0), (24, 36, 0, 2 * GQ, 0), (36, NF, 0, 3 * GQ, 0),
          (GQ, NF, GQ, 3 * GQ, NF - 36)]
GSLOTS = 12
NARR = 5
NPROD = 7
CH = 4
CHUNKS = D // CH

ALU = mybir.AluOpType
ACT = mybir.ActivationFunctionType
BF16 = mybir.dt.bfloat16
F32 = mybir.dt.float32
I32 = mybir.dt.int32

ARRAYS_OF = [(0, 1), (1, 2), (1, 3), (0, 2), (2, 3), (0, 3), (0, 4)]
LAST_USE = [max(k for k, of in enumerate(ARRAYS_OF) if a in of) for a in range(NARR)]
BASE_SETS = [(0, 1, 3, 10), (0, 4, 15, 20), (0, 6, 14, 27)]
LEFT_STEP = 17

WARM_UP = 9
LOOKUPS = 10
LOOKUP_PARTS = 8


def rows_each(rows):
    each = -(-rows // P)
    return each if rows % each == 0 else None


def looked_up(table_rows):
    fits = [f for f, rows in enumerate(table_rows) if rows_each(rows) and rows_each(rows) <= LOOKUP_PARTS]
    return fits[-LOOKUPS:]


def pieces():
    out = [(a, c * NF, base[a], NF) for a in range(1, 4) for c, base in enumerate(BASE_SETS)]
    return out + [(4, 0, LEFT_STEP, NF), (4, NF, 0, NF)]


def plan_products():
    fields = [[r % NF for r in range(KX)]] + [[None] * KX for _ in range(1, NARR)]
    for a, row, field, rows in pieces():
        fields[a][row:row + rows] = [(field + r) % NF for r in range(rows)]
    pair = [[(i, j) for i, j in zip(fields[a], fields[b]) if j is not None] for a, b in ARRAYS_OF]
    assert len({(min(p), max(p)) for rows in pair for p in rows}) == sum(map(len, pair)) == NF * (NF + 1) // 2
    return pair


ROWS_OF = [len(rows) for rows in plan_products()]


def constants():
    part = {"ident": np.eye(P, dtype=np.float32)}
    for each in range(1, LOOKUP_PARTS + 1):
        part[f"row{each}"] = (np.arange(P)[:, None] * each + np.arange(each)).astype(np.float32)
    part["mask"] = np.repeat((np.arange(P)[:, None] // D == np.arange(QUAD)).astype(np.float32), GI, 1)
    return part


def columns_of(part):
    at, out = 0, {}
    for name, a in part.items():
        out[name] = (at, at + a.shape[1])
        at += a.shape[1]
    return out, at


class Tile:

    def __init__(self, eng, reg, mul, add, slot, known, first=False, last=False):
        self.eng, self.reg, self.mul, self.add, self.known = eng, reg, mul, add, known
        self.slot, self.first, self.last = slot, first, last
        self.turn = None if last else PAIRS - 1 if first else PAIRS - 2

    def linear(self, by, plus):
        if self.reg is None:
            return by * self.add + plus
        key = (by * self.mul, by * self.add + plus)
        if key not in self.known:
            self.known[key] = self.eng.snap(self.reg * key[0] + key[1])
        return self.known[key]

    def pairs(self, q):
        return self.linear(PAIRS, q)

    def starts(self, q, back=1):
        return self.first and q < back

    def tiles(self, n):
        return self.linear(1, n)


def over_tiles(eng, body):
    body(Tile(eng, None, 0, 0, 0, {}, first=True))
    with eng.Fori(0, (TILES - 2) // 2) as it:
        known = {}
        body(Tile(eng, it, 2, 1, 1, known))
        body(Tile(eng, it, 2, 2, 0, known))
    body(Tile(eng, None, 0, TILES - 1, 1, {}, last=True))


def build(nc, ap, out):
    cols, ncols = columns_of(constants())
    table_rows = [ap[f"tbl_{f}"].shape[0] for f in range(NF)]
    lookups = looked_up(table_rows)

    with ExitStack() as ctx:
        def sb(name, shape, dt=F32):
            return ctx.enter_context(nc.sbuf_tensor(name, shape, dt))

        def bank(name):
            return ctx.enter_context(nc.psum_tensor(name, [P, 512], F32))

        def sem(name):
            return ctx.enter_context(nc.semaphore(name))

        const = sb("const", [P, ncols])
        w_pair = sb("w_pair", [P, NPROD, HALF])
        w_pair_turned = sb("w_pair_turned", [P, NPROD, HALF])
        w_layer2 = sb("w_layer2", [P, HM, K2])
        w_final1 = sb("w_final1", [P, GSLOTS, HALF])
        w_final1_turned = sb("w_final1_turned", [P, GSLOTS, HALF])
        w_top1_z2 = sb("w_top1_z2", [P, T1])
        w_top1_z1 = sb("w_top1_z1", [HALF + DC, T1])
        w_top2 = sb("w_top2", [P, T1 // P, T2])
        w_top3 = sb("w_top3", [P, T2 // P])
        b_top1 = sb("b_top1", [P, T1 // P])
        b_top2 = sb("b_top2", [P, T2 // P])

        ids = sb("ids", [P, TILES, NF], I32)
        ids_now = sb("ids_now", [P, 2, NF], I32)
        x = sb("x", [P, 2, NF, D])
        xt = sb("xt", [KX, 2, P * D])

        arrays = sb("arrays", [KX, NARR - 1, 2 * GT])
        prod = sb("prod", [P, 2, NPROD, 2 * GT])
        hidden_t = sb("hidden_t", [P, GT])
        hx = sb("hx", [P, 2, 2 * QUAD, GR])
        x_apart = sb("x_apart", [P, 2, 2 * QUAD, QUAD * GI])
        m_sum = sb("m_sum", [P, HM, P])
        g_sum = sb("g_sum", [P, GSLOTS, P])
        z2 = sb("z2", [P, P])
        z1_odd = sb("z1_odd", [HALF, P])
        z1_dense = sb("z1_dense", [HALF + DC, 2, P])
        h1 = sb("h1", [P, T1 // P, P])
        h2 = sb("h2", [P, T2 // P, P])
        y = sb("y", [1, 2, P])

        room = prod[:, :, :, :].rearrange("p s k n -> p (s k n)")
        places = [rows_each(table_rows[f]) * D for f in lookups]
        width = sum(places)

        def spread(of):
            return [of[0:table_rows[f] // rows_each(table_rows[f]), sum(places[:i]):sum(places[:i + 1])]
                    for i, f in enumerate(lookups)]

        tables = spread(room[:, 0:width])
        tables_rest = spread(room[:, width:2 * width])
        at = 2 * width
        table_parts = []
        for k in range(PARTS):
            table_parts.append(spread(room[:, at:at + width // 2].bitcast(BF16)))
            at += width // 2
        head_ids = room[:, at:at + len(lookups) * P]
        at += len(lookups) * P
        one_hot = [room[:, at + i * LOOKUP_PARTS * P // 2:at + (i + 1) * LOOKUP_PARTS * P // 2].bitcast(BF16)
                   for i in range(2)]
        head_ids_int = sb("head_ids_int", [P, len(lookups) * P], I32)

        acc = ctx.enter_context(nc.psum_tensor("acc", [P, 2, 512], F32))
        fresh = [bank("fresh0"), bank("fresh1")]
        turned = bank("turned")
        misc = bank("misc")
        gram = ctx.enter_context(nc.psum_tensor("gram", [P, 2, 512], F32))

        def cf(name):
            return const[:, cols[name][0]:cols[name][1]]

        s_ids = sem("s_ids")
        s_const = sem("s_const")
        s_wpair = sem("s_wpair")
        s_wlayer2 = sem("s_wlayer2")
        s_wtop = sem("s_wtop")
        s_dense = [sem("s_dense0"), sem("s_dense1")]
        gathered = [sem("gathered0"), sem("gathered1")]
        head_gathered = sem("head_gathered")
        zeroed = sem("zeroed")
        w_ready = sem("w_ready")
        final1_ready = sem("final1_ready")
        ids_copied = sem("ids_copied")
        gather_go = sem("gather_go")
        s_head_ids = sem("s_head_ids")
        s_table = [sem(f"s_table{i}") for i in range(len(lookups))]
        head_ids_ready = sem("head_ids_ready")
        table_hi = sem("table_hi")
        table_rest = sem("table_rest")
        table_mid = sem("table_mid")
        table_lo = sem("table_lo")
        one_hot_ready = sem("one_hot_ready")
        lookup_done = sem("lookup_done")
        looked_up_kept = sem("looked_up_kept")
        xtr_done = sem("xtr_done")
        xt_ready = sem("xt_ready")
        z_done = sem("z_done")
        z2_ready = sem("z2_ready")
        z1_ready = sem("z1_ready")
        h1_done = sem("h1_done")
        h1_ready = sem("h1_ready")
        h2_done = sem("h2_done")
        h2_ready = sem("h2_ready")
        y_done = sem("y_done")
        y_ready = sem("y_ready")
        y_out = sem("y_out")
        xt_copied = [sem(f"xt_copied{q}") for q in range(PAIRS)]
        array_ready = [None] + [sem(f"array_ready{a}") for a in range(1, NARR)]
        prod_ready = [sem(f"prod_ready{k}") for k in range(NPROD)]
        main_done = sem("main_done")
        hidden_ready = sem("hidden_ready")
        htt_done = sem("htt_done")
        hx_hidden = sem("hx_hidden")
        xsel_done = sem("xsel_done")
        hx_fields = sem("hx_fields")
        apart_ready = sem("apart_ready")
        gram_done = [sem("gram_done_a"), sem("gram_done_b")]
        last_kept = sem("last_kept")
        sums_kept = [sem("sums_kept_a"), sem("sums_kept_b")]

        def gather_count(n, t):
            if n.reg is None:
                return 16 * NF * ((n.add + t + 1) // 2)
            return n.eng.snap(n.reg * (16 * NF) + 16 * NF * ((n.add + t + 1) // 2))

        block = ctx.enter_context(nc.Block())

        @block.sync
        def _(sp):
            sp.dma_start(ids[:, :, :], ap["ids"].rearrange("(t p) f -> p t f", p=P)).then_inc(s_ids, 16)
            sp.dma_start(head_ids_int[:, :], ap["head_ids"].partition_broadcast(P)).then_inc(s_head_ids, 16)
            sp.dma_start(const[:, :], ap["const"]).then_inc(s_const, 16)
            for i, f in enumerate(lookups):
                sp.dma_start(tables[i], ap[f"tbl_{f}"].rearrange("(p c) d -> p (c d)", c=rows_each(table_rows[f])))\
                  .then_inc(s_table[i], 16)
            sp.dma_start(w_pair[:, :, :], ap["w_pair"]).then_inc(s_wpair, 16)
            sp.dma_start(w_pair_turned[:, :, :], ap["w_pair_turned"]).then_inc(s_wpair, 16)
            sp.dma_start(w_layer2[:, :, :], ap["w_layer2"]).then_inc(s_wlayer2, 16)
            sp.dma_start(w_final1[:, :, :], ap["w_final1"]).then_inc(s_wlayer2, 16)
            sp.dma_start(w_final1_turned[:, :, :], ap["w_final1_turned"]).then_inc(s_wlayer2, 16)
            sp.dma_start(w_top1_z1[0:HALF, :], ap["W_top1"][0:HALF, :]).then_inc(s_wtop, 16)
            sp.dma_start(w_top1_z2[:, :], ap["W_top1"][HALF:HALF + K2, :]).then_inc(s_wtop, 16)
            sp.dma_start(w_top1_z1[HALF:, :], ap["W_top1"][HALF + K2:, :]).then_inc(s_wtop, 16)
            sp.dma_start(w_top2[:, :, :], ap["W_top2"].rearrange("(k p) n -> p k n", p=P)).then_inc(s_wtop, 16)
            sp.dma_start(w_top3[:, :], ap["W_top3"]).then_inc(s_wtop, 16)
            sp.dma_start(b_top1[:, :], ap["b_top1"]).then_inc(s_wtop, 16)
            sp.dma_start(b_top2[:, :], ap["b_top2"]).then_inc(s_wtop, 16)

            both = 16 * (COPIES - 1)

            def copy_fields(n, q):
                tokens = slice(q * 2 * GT, (q + 1) * 2 * GT)
                for c in range(1, COPIES):
                    sp.dma_start(xt[c * NF:(c + 1) * NF, n.slot, tokens], xt[0:NF, n.slot, tokens])\
                      .then_inc(xt_copied[q], 16)

            def build_arrays(n, q, ahead=True):
                for i, (a, row, field, rows) in enumerate(pieces()):
                    if i == 1 and q + 1 < PAIRS and ahead:
                        sp.wait_ge(xt_copied[q + 1], n.linear(both, both))
                    elif not n.starts(q):
                        sp.wait_ge(prod_ready[LAST_USE[a]], n.pairs(q))
                    sp.dma_start(arrays[row:row + rows, a - 1, :],
                                 xt[field:field + rows, n.slot, q * 2 * GT:(q + 1) * 2 * GT]).then_inc(array_ready[a], 16)

            def tile(n):
                sp.wait_ge(xt_ready, n.linear(CHUNKS, CHUNKS + 1))
                copy_fields(n, 0)
                sp.wait_ge(xt_copied[0], n.linear(both, both))
                if n.first:
                    build_arrays(n, 0, ahead=False)
                    copy_fields(n, 1)
                    sp.wait_ge(xt_copied[1], both)
                else:
                    copy_fields(n, 1)
                    build_arrays(n, 0)
                copy_fields(n, 2)
                copy_fields(n, 3)
                for q in range(1, PAIRS):
                    build_arrays(n, q)

            over_tiles(sp, tile)
            sp.wait_ge(y_out, 16 * TILES)

        @block.gpsimd
        def _(pool):
            pool.wait_ge(s_ids, 16)

            def tile(n):
                if not n.first:
                    pool.wait_ge(xt_ready, n.linear(CHUNKS, 1 - CHUNKS))
                pool.tensor_copy(ids_now[:, n.slot, :], ids[:, bass.ds(n.tiles(0), 1), :].rearrange("p a f -> p (a f)"))\
                    .then_inc(ids_copied, 1)
                pool.wait_ge(ids_copied, n.tiles(1))
                pool.sem_inc(gather_go, 1)
                for f in range(NF):
                    if n.first and f in lookups:
                        continue
                    done = gathered[n.slot]
                    if n.first:
                        done = head_gathered
                    pool.indirect_dma_start(
                        out=x[:, n.slot, f, :], out_offset=None, in_=ap[f"tbl_{f}"],
                        in_offset=bass.IndirectOffsetOnAxis(ap=ids_now[:, n.slot, f:f + 1], axis=0),
                    ).then_inc(done, 16)

            over_tiles(pool, tile)

        @block.tensor
        def _(pe):
            def transposes(n, t, c):
                if n.reg is not None:
                    nc.tensor.transpose(fresh[c % 2][:, 0:P], x[:, (n.slot + t) % 2, 0:P // D, :].rearrange("p f d -> p (f d)"),
                                        cf("ident"))
                for i in range(CH):
                    last = nc.tensor.transpose(fresh[c % 2][0:NF, i * P:(i + 1) * P], x[:, (n.slot + t) % 2, :, c * CH + i],
                                               cf("ident"))
                last.then_inc(xtr_done, 1)

            def hidden(n, q, k):
                if k == 0 and not n.starts(q, back=2):
                    pe.wait_ge(hidden_ready, n.pairs(q - 1))
                pe.wait_ge(prod_ready[k], n.pairs(q + 1))
                rows = ROWS_OF[k]
                for g in range(2):
                    last = nc.tensor.matmul(acc[g * HALF:(g + 1) * HALF, q % 2, :], w_pair[0:rows, k, :],
                                            prod[0:rows, q % 2, k, g * GT:(g + 1) * GT],
                                            start=(k == 0), stop=(k == NPROD - 1))
                if k == NPROD - 1:
                    last.then_inc(main_done, 1)

            def turn_hidden(n, q):
                if not n.starts(q):
                    pe.wait_ge(hx_fields, n.pairs(q + 1))
                pe.wait_ge(hidden_ready, n.pairs(q + 1))
                for u in range(QUAD):
                    last = nc.tensor.transpose(turned[:, u * P:(u + 1) * P], hidden_t[:, u * P:(u + 1) * P], cf("ident"))
                last.then_inc(htt_done, 1)

            def turn_fields(n, q):
                for u in range(2 * QUAD):
                    at = q * 2 * GT + (u % 2) * GT + (u // 2) * P
                    last = nc.tensor.transpose(turned[:, u * GI:(u + 1) * GI], xt[0:NF, n.slot, at:at + P],
                                               cf("ident")[0:NF, 0:NF])
                last.then_inc(xsel_done, 1)

            def gram_sums(n, q, g, at_end=False):
                pe.wait_ge(hx_hidden, n.pairs(q + 1))
                pe.wait_ge(hx_fields, n.pairs(q + 1))
                pe.wait_ge(apart_ready, n.pairs(q + 1))
                sums = gram
                if at_end and g == 0:
                    sums = acc
                elif at_end:
                    pe.wait_ge(sums_kept[1], n.pairs(q))
                elif g == 1 or not n.starts(q):
                    pe.wait_ge(sums_kept[1 - g], n.pairs(q + g))
                for u in range(QUAD):
                    last = nc.tensor.matmul(sums[0:GR, u // 2, (u % 2) * QUAD * GI:(u % 2 + 1) * QUAD * GI],
                                            hx[:, q % 2, 2 * u + g, :], x_apart[:, q % 2, 2 * u + g, :],
                                            start=True, stop=True)
                last.then_inc(gram_done[g], 1)

            def layer2(n):
                pe.wait_ge(sums_kept[1], n.pairs(0))
                for m in range(HM):
                    nc.tensor.matmul(misc[:, 0:P], w_layer2[:, m, :], m_sum[:, m, :],
                                     start=(m == 0), stop=(m == HM - 1))
                for m in range(GSLOTS):
                    c = m % 2
                    last = nc.tensor.matmul(misc[c * HALF:(c + 1) * HALF, P:2 * P], w_final1[:, m, :],
                                            g_sum[:, m, :], start=(m < 2), stop=(m >= GSLOTS - 2))
                last.then_inc(z_done, 1)

            def tower1(n):
                slot = 1 - n.slot
                pe.wait_ge(z2_ready, n.tiles(0))
                pe.wait_ge(s_dense[slot], dense_loads(n))
                for c in range(T1 // P):
                    nc.tensor.matmul(misc[:, c * P:(c + 1) * P], w_top1_z2[:, c * P:(c + 1) * P], z2[:, :],
                                     start=True, stop=False)
                    if c == 0:
                        pe.wait_ge(z1_ready, n.tiles(0))
                    last = nc.tensor.matmul(misc[:, c * P:(c + 1) * P], w_top1_z1[:, c * P:(c + 1) * P],
                                            z1_dense[:, slot, :], start=False, stop=True)
                last.then_inc(h1_done, 1)

            def tower2(n):
                pe.wait_ge(h1_ready, n.tiles(0))
                for c in range(T2 // P):
                    for k in range(T1 // P):
                        last = nc.tensor.matmul(misc[:, c * P:(c + 1) * P], w_top2[:, k, c * P:(c + 1) * P], h1[:, k, :],
                                                start=(k == 0), stop=(k == T1 // P - 1))
                last.then_inc(h2_done, 1)

            def tower3(n):
                pe.wait_ge(h2_ready, n.tiles(0))
                for k in range(T2 // P):
                    last = nc.tensor.matmul(misc[0:1, 0:P], w_top3[:, k:k + 1], h2[:, k, :],
                                            start=(k == 0), stop=(k == T2 // P - 1))
                last.then_inc(y_done, 1)

            def dense_loads(n):
                if n.reg is None:
                    return 16 * ((n.add - 1) // 2 + 1)
                return n.eng.snap(n.reg * 16 + 16 * ((n.add - 1) // 2 + 1))

            for i, f in enumerate(lookups):
                rows, each = tables[i].shape[0], rows_each(table_rows[f])
                pe.wait_ge(one_hot_ready, i + 1)
                pe.wait_ge(table_lo, i + 1)
                for c in range(each):
                    for k in range(PARTS):
                        last = nc.tensor.matmul(acc[:, i % 2, (i // 2) * D:(i // 2 + 1) * D],
                                                one_hot[i % 2][0:rows, c * P:(c + 1) * P],
                                                table_parts[k][i][:, c * D:(c + 1) * D],
                                                start=(c == 0 and k == 0), stop=(c == each - 1 and k == PARTS - 1))
                last.then_inc(lookup_done, 1)
            for _ in range(WARM_UP):
                nc.tensor.matmul(fresh[0][:, 0:ncols], cf("ident"), const[:, :], start=True, stop=True)
            first = Tile(pe, None, 0, 0, 0, {}, first=True)
            pe.wait_ge(looked_up_kept, len(lookups))
            pe.wait_ge(head_gathered, 16 * (NF - len(lookups)))
            for c in range(CHUNKS):
                if c >= 2:
                    pe.wait_ge(xt_ready, c)
                transposes(first, 0, c)
            pe.wait_ge(w_ready, 1)
            pe.wait_ge(s_wlayer2, 3 * 16)
            pe.wait_ge(final1_ready, 1)
            pe.wait_ge(s_wtop, 7 * 16)

            def pair(n, q):
                tower = not n.first

                def chunk(c):
                    if n.turn and q == (n.turn if c >= CHUNKS // 2 else n.turn - 1):
                        if c == 0:
                            pe.wait_ge(gathered[1 - n.slot], gather_count(n, 1))
                        pe.wait_ge(xt_ready, n.linear(CHUNKS, CHUNKS + c))
                        transposes(n, 1, c)

                chunk(4)
                if not n.starts(q, back=2):
                    gram_sums(n, q - 2, 1)
                chunk(5)
                if not n.starts(q):
                    turn_hidden(n, q - 1)
                hidden(n, q, 0)
                chunk(6)
                hidden(n, q, 1)
                chunk(7)
                if tower and q == 3:
                    tower2(n)
                hidden(n, q, 2)
                if tower and q == 1:
                    layer2(n)
                if not n.starts(q):
                    gram_sums(n, q - 1, 0)
                turn_fields(n, q)
                chunk(0)
                hidden(n, q, 3)
                chunk(1)
                hidden(n, q, 4)
                chunk(2)
                hidden(n, q, 5)
                if tower and q == 1:
                    tower1(n)
                if tower and q == 3:
                    tower3(n)
                chunk(3)
                hidden(n, q, 6)

            def tile(n):
                for q in range(PAIRS):
                    pair(n, q)

            over_tiles(pe, tile)
            end = Tile(pe, None, 0, TILES, 0, {})
            gram_sums(end, -2, 1)
            turn_hidden(end, -1)
            gram_sums(end, -1, 0, at_end=True)
            pe.wait_ge(last_kept, 1)
            gram_sums(end, -1, 1, at_end=True)
            pe.wait_ge(last_kept, 3)
            layer2(end)
            pe.wait_ge(z2_ready, end.tiles(0))
            tower1(end)
            tower2(end)
            tower3(end)

        @block.scalar
        def _(act):
            copy = ACT.Copy
            act.wait_ge(s_head_ids, 16)
            nc.scalar.activation(head_ids, head_ids_int[:, :], copy).then_inc(head_ids_ready, 1)

            def keep_transposes(n, t, c):
                slot = (n.slot + t) % 2
                act.wait_ge(xtr_done, n.linear(CHUNKS, CHUNKS * t + c + 1))
                if c == 0 and not n.first:
                    act.wait_ge(prod_ready[NPROD - 1], n.pairs(0))
                    act.wait_ge(xsel_done, n.pairs(0))
                at = xt[0:NF, slot, :].rearrange("p (b d) -> p b d", d=D)[:, :, c * CH:(c + 1) * CH]
                nc.scalar.activation(at, fresh[c % 2][0:NF, :].rearrange("p (d b) -> p b d", d=CH), copy).then_inc(xt_ready, 1)

            def keep_hidden(n, q):
                act.wait_ge(main_done, n.pairs(q + 1))
                nc.scalar.activation(hidden_t[:, :], acc[:, q % 2, :], copy).then_inc(hidden_ready, 1)

            def keep_turned_hidden(n, q):
                act.wait_ge(htt_done, n.pairs(q + 1))
                nc.scalar.activation(hx[:, q % 2, :, 0:HALF], turned[:, :].rearrange("p (u j) -> p u j", j=HALF), copy)\
                    .then_inc(hx_hidden, 1)

            def keep_fields(n, q):
                act.wait_ge(xsel_done, n.pairs(q + 1))
                nc.scalar.activation(hx[:, q % 2, :, HALF:GR],
                                     turned[:, 0:2 * QUAD * GI].rearrange("p (u i) -> p u i", i=GI), copy)\
                    .then_inc(hx_fields, 1)

            def keep_sums(n, q, g, blocks=BLOCKS, of=gram):
                act.wait_ge(gram_done[g], n.pairs(q + 1))
                src = of[:, :, 0:2 * QUAD * GI].rearrange("p h (b i) -> p h b i", i=GI)
                at = (q % PAIRS) * 2 * GB + g * GB
                for half, fields in enumerate(IN_HALF):
                    to = m_sum[half * HALF:(half + 1) * HALF, 0:fields, at:at + GB]
                    last = nc.scalar.activation(to.rearrange("p m (h b) -> p h b m", h=2),
                                                src[0:HALF, :, :, half * HM:half * HM + fields], copy)
                for lo, hi, row, part, slot in blocks:
                    rows = min(GQ, NF - row)
                    to = g_sum[part:part + rows, slot:slot + hi - lo, at:at + GB]
                    last = nc.scalar.activation(to.rearrange("p m (h b) -> p h b m", h=2),
                                                src[HALF + row:HALF + row + rows, :, :, lo:hi], copy)
                last.then_inc(sums_kept[g], 1)

            def keep_z(n):
                act.wait_ge(z_done, n.tiles(0))
                nc.scalar.activation(z1_odd[:, :], misc[HALF:P, P:2 * P], copy)
                nc.scalar.activation(z1_dense[0:HALF, 1 - n.slot, :], misc[0:HALF, P:2 * P], copy)
                nc.scalar.activation(z2[:, :], misc[:, 0:P], copy).then_inc(z2_ready, 1)

            def relu1(n):
                act.wait_ge(h1_done, n.tiles(0))
                for c in range(T1 // P):
                    last = nc.scalar.activation(h1[:, c, :], misc[:, c * P:(c + 1) * P], ACT.Relu,
                                                bias=b_top1[:, c:c + 1])
                last.then_inc(h1_ready, 1)

            def relu2(n):
                act.wait_ge(h2_done, n.tiles(0))
                for c in range(T2 // P):
                    last = nc.scalar.activation(h2[:, c, :], misc[:, c * P:(c + 1) * P], ACT.Relu,
                                                bias=b_top2[:, c:c + 1])
                last.then_inc(h2_ready, 1)

            def keep_y(n):
                act.wait_ge(y_done, n.tiles(0))
                nc.scalar.activation(y[0:1, 1 - n.slot, :], misc[0:1, 0:P], copy).then_inc(y_ready, 1)

            def load_dense(n):
                act.dma_start(z1_dense[HALF:, n.slot, :], ap["dense_t"][:, bass.ds(n.linear(P, 0), P)])\
                   .then_inc(s_dense[n.slot], 16)

            def store_y(n):
                act.wait_ge(y_ready, n.tiles(0))
                act.dma_start(out[:, bass.ds(n.linear(P, -P), P)], y[0:1, 1 - n.slot, :]).then_inc(y_out, 16)

            for i in range(len(lookups)):
                act.wait_ge(s_table[i], 16)
                nc.scalar.activation(table_parts[0][i], tables[i], copy).then_inc(table_hi, 1)
                act.wait_ge(table_rest, i + 1)
                nc.scalar.activation(table_parts[1][i], tables_rest[i], copy).then_inc(table_mid, 1)
            act.wait_ge(lookup_done, len(lookups))
            for i, f in enumerate(lookups):
                nc.scalar.activation(x[:, 0, f, :], acc[:, i % 2, (i // 2) * D:(i // 2 + 1) * D], copy)\
                  .then_inc(looked_up_kept, 1)
            first = Tile(act, None, 0, 0, 0, {}, first=True)
            act.wait_ge(zeroed, 2)
            for c in range(CHUNKS):
                keep_transposes(first, 0, c)
            act.wait_ge(s_wtop, 7 * 16)

            def pair(n, q):
                tower = not n.first

                def chunk(c):
                    if n.turn and q == (n.turn if c >= CHUNKS // 2 else n.turn - 1):
                        keep_transposes(n, 1, c)

                if q == 0:
                    load_dense(n)
                if not n.starts(q):
                    keep_hidden(n, q - 1)
                chunk(4)
                chunk(5)
                if not n.starts(q):
                    keep_turned_hidden(n, q - 1)
                if not n.starts(q, back=2):
                    keep_sums(n, q - 2, 1)
                chunk(6)
                chunk(7)
                if tower and q == 3:
                    relu2(n)
                if tower and q == 1:
                    keep_z(n)
                keep_fields(n, q)
                chunk(0)
                if not n.starts(q):
                    keep_sums(n, q - 1, 0)
                chunk(1)
                chunk(2)
                if tower and q == 1:
                    relu1(n)
                if tower and q == 3:
                    keep_y(n)
                    store_y(n)
                chunk(3)

            def tile(n):
                for q in range(PAIRS):
                    pair(n, q)

            over_tiles(act, tile)
            end = Tile(act, None, 0, TILES, 0, {})
            keep_hidden(end, -1)
            keep_turned_hidden(end, -1)
            keep_sums(end, -2, 1, [])
            keep_sums(end, -1, 0, [], acc)
            keep_sums(end, -1, 1, [])
            keep_z(end)
            relu1(end)
            relu2(end)
            keep_y(end)
            store_y(end)

        @block.vector
        def _(dve):
            nc.vector.memset(m_sum[:, HM - 1, :], 0.0).then_inc(zeroed, 1)
            nc.vector.memset(g_sum[:, :, :], 0.0).then_inc(zeroed, 1)
            nc.vector.memset(h2[:, 0, 0:1], 0.0).then_inc(xt_ready, 1)

            def match_ids(i):
                each = rows_each(table_rows[lookups[i]])
                rows = tables[i].shape[0]
                if i >= 2:
                    dve.wait_ge(lookup_done, i - 1)
                its = head_ids[0:rows, i * P:(i + 1) * P].rearrange("p (c b) -> p c b", c=1).to_broadcast([rows, each, P])
                row = cf(f"row{each}")[0:rows, :].rearrange("p (c b) -> p c b", b=1).to_broadcast([rows, each, P])
                nc.vector.tensor_tensor(one_hot[i % 2][0:rows, 0:each * P].rearrange("p (c b) -> p c b", c=each),
                                        its, row, ALU.is_equal).then_inc(one_hot_ready, 1)

            dve.wait_ge(s_const, 16)
            dve.wait_ge(head_ids_ready, 1)
            for i in range(len(lookups)):
                dve.wait_ge(table_hi, i + 1)
                nc.vector.tensor_tensor(tables_rest[i], tables[i], table_parts[0][i], ALU.subtract).then_inc(table_rest, 1)
                match_ids(i)
                dve.wait_ge(table_mid, i + 1)
                nc.vector.tensor_tensor(table_parts[2][i], tables_rest[i], table_parts[1][i], ALU.subtract)\
                  .then_inc(table_lo, 1)
            dve.wait_ge(s_wpair, 2 * 16)
            nc.vector.tensor_tensor(w_pair[:, :, :], w_pair[:, :, :], w_pair_turned[:, :, :], ALU.add).then_inc(w_ready, 1)
            dve.wait_ge(s_wlayer2, 3 * 16)
            nc.vector.tensor_tensor(w_final1[:, :, :], w_final1[:, :, :], w_final1_turned[:, :, :], ALU.add)\
              .then_inc(final1_ready, 1)

            def multiply(n, q, k0, k1):
                tile_of, pair_of = divmod(q, PAIRS)
                slot = (n.slot + tile_of) % 2
                both = 16 * (COPIES - 1)
                dve.wait_ge(xt_copied[pair_of], n.linear(both, both * (tile_of + 1)))
                if not n.starts(q, back=2):
                    dve.wait_ge(main_done, n.pairs(q - 1))
                for k in range(k0, k1):
                    rows = ROWS_OF[k]
                    operands = []
                    for of in ARRAYS_OF[k]:
                        if of:
                            loads = 16 * len([p for p in pieces() if p[0] == of])
                            dve.wait_ge(array_ready[of], n.linear(PAIRS * loads, (q + 1) * loads))
                            operands.append(arrays[0:rows, of - 1, :])
                        else:
                            operands.append(xt[0:rows, slot, pair_of * 2 * GT:(pair_of + 1) * 2 * GT])
                    nc.vector.tensor_tensor(prod[0:rows, q % 2, k, :], *operands, ALU.mult).then_inc(prod_ready[k], 1)

            def set_apart(n, q):
                dve.wait_ge(hx_fields, n.pairs(q + 1))
                src = hx[:, q % 2, :, HALF:GR]
                mask = cf("mask").rearrange("p (b i) -> p b i", i=GI)
                for b in range(QUAD):
                    last = nc.vector.tensor_tensor(
                        x_apart[:, q % 2, :, b * GI:(b + 1) * GI], src,
                        mask[:, b:b + 1, :].to_broadcast([P, 2 * QUAD, GI]), ALU.mult)
                last.then_inc(apart_ready, 1)

            def add_z1(n):
                dve.wait_ge(z2_ready, n.tiles(0))
                z1 = z1_dense[0:HALF, 1 - n.slot, :]
                nc.vector.tensor_tensor(z1, z1, z1_odd[:, :], ALU.add)\
                  .then_inc(z1_ready, 1)

            multiply(Tile(dve, None, 0, 0, 0, {}, first=True), 0, 0, NPROD)

            def pair(n, q):
                more = not (n.last and q == PAIRS - 1)
                if q == PAIRS - 1:
                    set_apart(n, q)
                    if more:
                        multiply(n, q + 1, 0, NPROD)
                else:
                    multiply(n, q + 1, 0, 5)
                    if not n.first and q == 1:
                        add_z1(n)
                    set_apart(n, q)
                    multiply(n, q + 1, 5, NPROD)

            def tile(n):
                for q in range(PAIRS):
                    pair(n, q)

            over_tiles(dve, tile)
            end = Tile(dve, None, 0, TILES, 0, {})
            for q, g, of in ((-2, 1, gram), (-1, 0, acc), (-1, 1, gram)):
                dve.wait_ge(gram_done[g], end.pairs(q + 1))
                src = of[:, :, 0:2 * QUAD * GI].rearrange("p h (b i) -> p h b i", i=GI)
                at = (q % PAIRS) * 2 * GB + g * GB
                for lo, hi, row, part, slot in BLOCKS:
                    rows = min(GQ, NF - row)
                    to = g_sum[part:part + rows, slot:slot + hi - lo, at:at + GB]
                    last = nc.vector.tensor_copy(to.rearrange("p m (h b) -> p h b m", h=2),
                                                 src[HALF + row:HALF + row + rows, :, :, lo:hi])
                last.then_inc(last_kept, 1)
            add_z1(end)


def kernel(**inputs):
    import concourse.bacc as bacc
    from concourse.bass_utils import run_bass_kernel_spmd

    def rows(a):
        return np.asarray(a)

    lookups = looked_up([inputs[f"tbl_{f}"].shape[0] for f in range(NF)])
    w1 = rows(inputs["L0_rec_W1"]).reshape(NF, NF, K1)
    w_pair = np.zeros((P, NPROD, HALF), np.float32)
    w_pair_turned = np.zeros((P, NPROD, HALF), np.float32)
    for t, held in enumerate(plan_products()):
        for r, (i, j) in enumerate(held):
            w_pair[r, t] = w1[i, j, :HALF]
            if i != j:
                w_pair_turned[r, t] = w1[j, i, :HALF]
    w2 = rows(inputs["L0_rec_W2"]).reshape(NF, HALF, K2)
    w_layer2 = np.zeros((P, HM, K2), np.float32)
    for i in range(NF):
        par, m = i // HM, i % HM
        w_layer2[par * HALF:(par + 1) * HALF, m] = w2[i]
    w_final1 = np.zeros((P, GSLOTS, HALF), np.float32)
    w_final1_turned = np.zeros((P, GSLOTS, HALF), np.float32)
    for lo, hi, row, part, slot in BLOCKS:
        of = list(range(row, min(row + GQ, NF)))
        for c in range(lo, hi):
            w_final1[part:part + len(of), slot + c - lo] = w1[c, of, HALF:]
            if c >= GQ and row == 0:
                w_final1_turned[part:part + len(of), slot + c - lo] = w1[of, c, HALF:]
    arrays = {
        "ids": rows(inputs["ids"]),
        "head_ids": np.ascontiguousarray(rows(inputs["ids"])[:P, lookups].T).reshape(-1),
        "const": np.concatenate(list(constants().values()), 1),
        "w_pair": w_pair, "w_pair_turned": w_pair_turned, "w_layer2": w_layer2, "w_final1": w_final1,
        "w_final1_turned": w_final1_turned,
        "W_top1": rows(inputs["W_top1"]), "W_top2": rows(inputs["W_top2"]),
        "W_top3": np.ascontiguousarray(rows(inputs["W_top3"]).reshape(T2 // P, P).T),
        "b_top1": np.ascontiguousarray(rows(inputs["b_top1"]).reshape(T1 // P, P).T),
        "b_top2": np.ascontiguousarray(rows(inputs["b_top2"]).reshape(T2 // P, P).T),
        "dense_t": np.ascontiguousarray(rows(inputs["dense_ctx"]).T),
    }
    for f in range(NF):
        arrays[f"tbl_{f}"] = rows(inputs[f"tbl_{f}"])

    nc = bacc.Bacc("TRN2", target_bir_lowering=False, num_devices=1)
    ap = {k: nc.dram_tensor(f"in_{k}", a.shape, mybir.dt.from_np(a.dtype), kind="ExternalInput").ap()
          for k, a in arrays.items()}
    out = nc.dram_tensor("out", (1, B), F32, kind="ExternalOutput").ap()
    build(nc, ap, out)
    r = run_bass_kernel_spmd(nc, [{f"in_{k}": a for k, a in arrays.items()}], core_ids=[0])
    return r.results[0]["out"].reshape(B, 1)
```
